# Optimizing a Trainium2 kernel written in Bass

```python
import numpy as np
import jax
import jax.numpy as jnp

def _softmax(x, axis=-1):
    return jax.nn.softmax(x, axis=axis)

def _gelu(x):
    return jax.nn.gelu(x, approximate=True)

def _silu(x):
    return jax.nn.silu(x)

def _sigmoid(x):
    return jax.nn.sigmoid(x)

def _layernorm(x, axis=-1, eps=1e-05):
    m = jnp.mean(x, axis=axis, keepdims=True)
    v = jnp.var(x, axis=axis, keepdims=True)
    return (x - m) / jnp.sqrt(v + eps)

def _scatter_add(tgt, idx, src, axis=0):
    return tgt.at[idx].add(src)

def _segment_sum(src, seg, n):
    return jax.ops.segment_sum(src, seg, n)
kernel_name = 'mk_cond_seq_d4_seqx_r4_53c734'

def setup_inputs(seed: int=0):
    np.random.seed(seed)
    _w = jnp.asarray

    def _rec_inputs():
        import jax
        import jax.numpy as jnp
        _rk = jax.random.key(seed)
        x = 0.5 + 0.2887 * jax.random.normal(jax.random.fold_in(_rk, 1), (32, 64, 512), jnp.float32)
        _lenS = 64 - jax.random.randint(jax.random.fold_in(_rk, 7), (32,), 0, max(1, 64 // 4) + 1, jnp.int32)
        _lenS2 = 64 - jax.random.randint(jax.random.fold_in(_rk, 8), (32,), 0, max(1, 64 // 4) + 1, jnp.int32)
        itok_B_17_1546 = jax.random.randint(jax.random.fold_in(_rk, 12), (32,), 17, 1547, jnp.int32)
        itok_B_1_2 = jax.random.randint(jax.random.fold_in(_rk, 13), (32,), 1, 3, jnp.int32)
        return (x, itok_B_17_1546, itok_B_1_2, _lenS)
    x, itok_B_17_1546, itok_B_1_2, _lenS = _rec_inputs()

    def _L0_cond_setup():
        import jax, jax.numpy as jnp
        import numpy as np
        B, T, V = (8, 128, 512)
        H = 4 * V
        key = jax.random.key(seed)
        ks = jax.random.split(key, 16)
        s = lambda n: 1.0 / np.sqrt(n)
        inp = {'x': jax.random.uniform(ks[0], (B, T, V), dtype=jnp.float32), 'lens': jax.random.randint(ks[1], (B,), 1, T, dtype=jnp.int64), 'target_codes': jax.random.randint(ks[2], (B,), 0, V, dtype=jnp.int64), 'Wq': jax.random.normal(ks[3], (V, V), jnp.float32) * s(V), 'Wk': jax.random.normal(ks[4], (V, V), jnp.float32) * s(V), 'Wv': jax.random.normal(ks[5], (V, V), jnp.float32) * s(V), 'Wp': jax.random.normal(ks[6], (V, V), jnp.float32) * s(V), 'bp': jnp.zeros((V,), jnp.float32), 'cW1': jax.random.normal(ks[7], (V, H), jnp.float32) * s(V), 'cb1': jnp.zeros((H,), jnp.float32), 'cW2': jax.random.normal(ks[8], (H, V), jnp.float32) * s(H), 'cb2': jnp.zeros((V,), jnp.float32), 'mW1': jax.random.normal(ks[9], (2 * V, H), jnp.float32) * s(2 * V), 'mb1': jnp.zeros((H,), jnp.float32), 'mW2': jax.random.normal(ks[10], (H, V), jnp.float32) * s(H), 'mb2': jnp.zeros((V,), jnp.float32)}
        return inp
    _L0_cond_all = _L0_cond_setup()
    _L0_cond_in = {k: v for k, v in _L0_cond_all.items() if k in ('Wq', 'Wk', 'Wv', 'Wp', 'bp', 'cW1', 'cb1', 'cW2', 'cb2', 'mW1', 'mb1', 'mW2', 'mb2')}
    del _L0_cond_all

    def _L1_cond_setup():
        import jax, jax.numpy as jnp
        import numpy as np
        H = 512
        K = 256
        R = 3
        B = 8
        S = 512
        LN_EPS = 1e-05
        key = jax.random.key(seed)
        ks = jax.random.split(key, 8)
        sd_d = 1.0 / np.sqrt(H)
        sd_u = 1.0 / np.sqrt(K)
        return {'role': jax.random.randint(ks[0], (B,), 0, R), 'hidden_states': jax.random.normal(ks[1], (B, S, H), dtype=jnp.float32), 'W_down': jax.random.uniform(ks[2], (R, H, K), jnp.float32, -sd_d, sd_d), 'b_down': jax.random.uniform(ks[3], (R, K), jnp.float32, -sd_d, sd_d), 'W_up': jax.random.uniform(ks[4], (R, K, H), jnp.float32, -sd_u, sd_u), 'b_up': jax.random.uniform(ks[5], (R, H), jnp.float32, -sd_u, sd_u), 'gamma': jnp.ones((R, H), jnp.float32), 'beta': jnp.zeros((R, H), jnp.float32)}
    _L1_cond_all = _L1_cond_setup()
    _L1_cond_in = {k: v for k, v in _L1_cond_all.items() if k in ('W_down', 'b_down', 'W_up', 'b_up', 'gamma', 'beta')}
    del _L1_cond_all

    def _L2_cond_setup():
        import jax, jax.numpy as jnp
        import numpy as np
        B, T, V = (8, 128, 512)
        H = 4 * V
        key = jax.random.key(seed)
        ks = jax.random.split(key, 16)
        s = lambda n: 1.0 / np.sqrt(n)
        inp = {'x': jax.random.uniform(ks[0], (B, T, V), dtype=jnp.float32), 'lens': jax.random.randint(ks[1], (B,), 1, T, dtype=jnp.int64), 'target_codes': jax.random.randint(ks[2], (B,), 0, V, dtype=jnp.int64), 'Wq': jax.random.normal(ks[3], (V, V), jnp.float32) * s(V), 'Wk': jax.random.normal(ks[4], (V, V), jnp.float32) * s(V), 'Wv': jax.random.normal(ks[5], (V, V), jnp.float32) * s(V), 'Wp': jax.random.normal(ks[6], (V, V), jnp.float32) * s(V), 'bp': jnp.zeros((V,), jnp.float32), 'cW1': jax.random.normal(ks[7], (V, H), jnp.float32) * s(V), 'cb1': jnp.zeros((H,), jnp.float32), 'cW2': jax.random.normal(ks[8], (H, V), jnp.float32) * s(H), 'cb2': jnp.zeros((V,), jnp.float32), 'mW1': jax.random.normal(ks[9], (2 * V, H), jnp.float32) * s(2 * V), 'mb1': jnp.zeros((H,), jnp.float32), 'mW2': jax.random.normal(ks[10], (H, V), jnp.float32) * s(H), 'mb2': jnp.zeros((V,), jnp.float32)}
        return inp
    _L2_cond_all = _L2_cond_setup()
    _L2_cond_in = {k: v for k, v in _L2_cond_all.items() if k in ('Wq', 'Wk', 'Wv', 'Wp', 'bp', 'cW1', 'cb1', 'cW2', 'cb2', 'mW1', 'mb1', 'mW2', 'mb2')}
    del _L2_cond_all

    def _L3_cond_setup():
        import jax, jax.numpy as jnp
        import numpy as np
        B, S, H = (8, 512, 512)
        BN = 256
        E = 3
        LN_EPS = 1e-05
        key = jax.random.key(seed)
        ks = jax.random.split(key, 8)
        stream = jax.random.randint(ks[0], (B,), 0, E, dtype=jnp.int32)
        hidden_states = jax.random.normal(ks[1], (B, S, H), dtype=jnp.float32)
        W_down = jax.random.normal(ks[2], (E, H, BN), dtype=jnp.float32) * 0.02
        b_down = jnp.zeros((E, BN), dtype=jnp.float32)
        W_up = jax.random.normal(ks[3], (E, BN, H), dtype=jnp.float32) * 0.02
        b_up = jnp.zeros((E, H), dtype=jnp.float32)
        ln_w = jnp.ones((E, H), dtype=jnp.float32)
        ln_b = jnp.zeros((E, H), dtype=jnp.float32)
        return {'stream': stream, 'hidden_states': hidden_states, 'W_down': W_down, 'b_down': b_down, 'W_up': W_up, 'b_up': b_up, 'ln_w': ln_w, 'ln_b': ln_b}
    _L3_cond_all = _L3_cond_setup()
    _L3_cond_in = {k: v for k, v in _L3_cond_all.items() if k in ('W_down', 'b_down', 'W_up', 'b_up', 'ln_w', 'ln_b')}
    del _L3_cond_all
    return {'x': x, 'itok_B_17_1546': itok_B_17_1546, 'itok_B_1_2': itok_B_1_2, '_lenS': _lenS, 'L0_cond_Wq': _L0_cond_in['Wq'], 'L0_cond_Wk': _L0_cond_in['Wk'], 'L0_cond_Wv': _L0_cond_in['Wv'], 'L0_cond_Wp': _L0_cond_in['Wp'], 'L0_cond_bp': _L0_cond_in['bp'], 'L0_cond_cW1': _L0_cond_in['cW1'], 'L0_cond_cb1': _L0_cond_in['cb1'], 'L0_cond_cW2': _L0_cond_in['cW2'], 'L0_cond_cb2': _L0_cond_in['cb2'], 'L0_cond_mW1': _L0_cond_in['mW1'], 'L0_cond_mb1': _L0_cond_in['mb1'], 'L0_cond_mW2': _L0_cond_in['mW2'], 'L0_cond_mb2': _L0_cond_in['mb2'], 'L1_cond_W_down': _L1_cond_in['W_down'], 'L1_cond_b_down': _L1_cond_in['b_down'], 'L1_cond_W_up': _L1_cond_in['W_up'], 'L1_cond_b_up': _L1_cond_in['b_up'], 'L1_cond_gamma': _L1_cond_in['gamma'], 'L1_cond_beta': _L1_cond_in['beta'], 'L2_cond_Wq': _L2_cond_in['Wq'], 'L2_cond_Wk': _L2_cond_in['Wk'], 'L2_cond_Wv': _L2_cond_in['Wv'], 'L2_cond_Wp': _L2_cond_in['Wp'], 'L2_cond_bp': _L2_cond_in['bp'], 'L2_cond_cW1': _L2_cond_in['cW1'], 'L2_cond_cb1': _L2_cond_in['cb1'], 'L2_cond_cW2': _L2_cond_in['cW2'], 'L2_cond_cb2': _L2_cond_in['cb2'], 'L2_cond_mW1': _L2_cond_in['mW1'], 'L2_cond_mb1': _L2_cond_in['mb1'], 'L2_cond_mW2': _L2_cond_in['mW2'], 'L2_cond_mb2': _L2_cond_in['mb2'], 'L3_cond_W_down': _L3_cond_in['W_down'], 'L3_cond_b_down': _L3_cond_in['b_down'], 'L3_cond_W_up': _L3_cond_in['W_up'], 'L3_cond_b_up': _L3_cond_in['b_up'], 'L3_cond_ln_w': _L3_cond_in['ln_w'], 'L3_cond_ln_b': _L3_cond_in['ln_b']}

def reference(x, itok_B_17_1546, itok_B_1_2, _lenS, L0_cond_Wq, L0_cond_Wk, L0_cond_Wv, L0_cond_Wp, L0_cond_bp, L0_cond_cW1, L0_cond_cb1, L0_cond_cW2, L0_cond_cb2, L0_cond_mW1, L0_cond_mb1, L0_cond_mW2, L0_cond_mb2, L1_cond_W_down, L1_cond_b_down, L1_cond_W_up, L1_cond_b_up, L1_cond_gamma, L1_cond_beta, L2_cond_Wq, L2_cond_Wk, L2_cond_Wv, L2_cond_Wp, L2_cond_bp, L2_cond_cW1, L2_cond_cb1, L2_cond_cW2, L2_cond_cb2, L2_cond_mW1, L2_cond_mb1, L2_cond_mW2, L2_cond_mb2, L3_cond_W_down, L3_cond_b_down, L3_cond_W_up, L3_cond_b_up, L3_cond_ln_w, L3_cond_ln_b):
    import jax
    import jax.numpy as jnp

    def _L0_cond_ref(x, lens, target_codes, Wq, Wk, Wv, Wp, bp, cW1, cb1, cW2, cb2, mW1, mb1, mW2, mb2):
        import jax, jax.numpy as jnp
        import numpy as np
        B, T, V = (8, 128, 512)
        H = 4 * V
        scale = V ** (-0.5)
        q = x @ Wq
        k = x @ Wk
        v = x @ Wv
        attn = jnp.einsum('btd,bTd->btT', q, k) * scale
        attn = jax.nn.softmax(attn, axis=-1)
        attn_out = jnp.einsum('btT,bTd->btd', attn, v) @ Wp + bp
        target_embed = jax.nn.one_hot(target_codes, V, dtype=x.dtype)[:, None, :]
        cms_out = jax.nn.gelu(attn_out @ cW1 + cb1, approximate=False) @ cW2 + cb2
        cms_out = cms_out + target_embed
        concat = jnp.concatenate([attn_out, cms_out], axis=-1)
        modifier = jax.nn.gelu(concat @ mW1 + mb1, approximate=False) @ mW2 + mb2
        out = jnp.clip(x + cms_out + modifier, 0.0, 1.0)
        return out

    def _L1_cond_ref(role, hidden_states, W_down, b_down, W_up, b_up, gamma, beta):
        import jax, jax.numpy as jnp
        import numpy as np
        H = 512
        K = 256
        R = 3
        B = 8
        S = 512
        LN_EPS = 1e-05
        h = jnp.einsum('bsh,bhk->bsk', hidden_states, W_down[role]) + b_down[role][:, None, :]
        h = jax.nn.gelu(h, approximate=False)
        u = jnp.einsum('bsk,bkh->bsh', h, W_up[role]) + b_up[role][:, None, :]
        y = hidden_states + u
        mean = jnp.mean(y, axis=-1, keepdims=True)
        var = jnp.mean(jnp.square(y - mean), axis=-1, keepdims=True)
        yn = (y - mean) * jax.lax.rsqrt(var + LN_EPS)
        return yn * gamma[role][:, None, :] + beta[role][:, None, :]

    def _L2_cond_ref(x, lens, target_codes, Wq, Wk, Wv, Wp, bp, cW1, cb1, cW2, cb2, mW1, mb1, mW2, mb2):
        import jax, jax.numpy as jnp
        import numpy as np
        B, T, V = (8, 128, 512)
        H = 4 * V
        scale = V ** (-0.5)
        q = x @ Wq
        k = x @ Wk
        v = x @ Wv
        attn = jnp.einsum('btd,bTd->btT', q, k) * scale
        attn = jax.nn.softmax(attn, axis=-1)
        attn_out = jnp.einsum('btT,bTd->btd', attn, v) @ Wp + bp
        target_embed = jax.nn.one_hot(target_codes, V, dtype=x.dtype)[:, None, :]
        cms_out = jax.nn.gelu(attn_out @ cW1 + cb1, approximate=False) @ cW2 + cb2
        cms_out = cms_out + target_embed
        concat = jnp.concatenate([attn_out, cms_out], axis=-1)
        modifier = jax.nn.gelu(concat @ mW1 + mb1, approximate=False) @ mW2 + mb2
        out = jnp.clip(x + cms_out + modifier, 0.0, 1.0)
        return out

    def _L3_cond_ref(stream, hidden_states, W_down, b_down, W_up, b_up, ln_w, ln_b):
        import jax, jax.numpy as jnp
        import numpy as np
        B, S, H = (8, 512, 512)
        BN = 256
        E = 3
        LN_EPS = 1e-05
        Wd = W_down[stream]
        bd = b_down[stream]
        Wu = W_up[stream]
        bu = b_up[stream]
        g = ln_w[stream]
        b = ln_b[stream]
        residual = hidden_states
        h = jnp.einsum('bsh,bhk->bsk', hidden_states, Wd) + bd[:, None, :]
        h = jax.nn.gelu(h, approximate=False)
        h = jnp.einsum('bsk,bkh->bsh', h, Wu) + bu[:, None, :]
        h = residual + h
        mean = jnp.mean(h, axis=-1, keepdims=True)
        var = jnp.mean(jnp.square(h - mean), axis=-1, keepdims=True)
        h = (h - mean) * jax.lax.rsqrt(var + LN_EPS)
        return h * g[:, None, :] + b[:, None, :]
    x = _L0_cond_ref(x, _lenS, itok_B_17_1546, L0_cond_Wq, L0_cond_Wk, L0_cond_Wv, L0_cond_Wp, L0_cond_bp, L0_cond_cW1, L0_cond_cb1, L0_cond_cW2, L0_cond_cb2, L0_cond_mW1, L0_cond_mb1, L0_cond_mW2, L0_cond_mb2)
    x = _L1_cond_ref(itok_B_1_2, x, L1_cond_W_down, L1_cond_b_down, L1_cond_W_up, L1_cond_b_up, L1_cond_gamma, L1_cond_beta)
    x = _L2_cond_ref(x, _lenS, itok_B_17_1546, L2_cond_Wq, L2_cond_Wk, L2_cond_Wv, L2_cond_Wp, L2_cond_bp, L2_cond_cW1, L2_cond_cb1, L2_cond_cW2, L2_cond_cb2, L2_cond_mW1, L2_cond_mb1, L2_cond_mW2, L2_cond_mb2)
    x = _L3_cond_ref(itok_B_1_2, x, L3_cond_W_down, L3_cond_b_down, L3_cond_W_up, L3_cond_b_up, L3_cond_ln_w, L3_cond_ln_b)
    return x

_drawn_inputs = setup_inputs


def setup_inputs(seed=0):
    import zlib

    import numpy as np

    out = dict(_drawn_inputs(seed))
    spreads = {'L0_cond_bp': (0.0, 0.1),
     'L0_cond_cb1': (0.0, 0.1),
     'L0_cond_cb2': (0.0, 0.1),
     'L0_cond_mb1': (0.0, 0.1),
     'L0_cond_mb2': (0.0, 0.1),
     'L1_cond_gamma': (1.0, 0.2),
     'L1_cond_beta': (0.0, 0.1),
     'L2_cond_bp': (0.0, 0.1),
     'L2_cond_cb1': (0.0, 0.1),
     'L2_cond_cb2': (0.0, 0.1),
     'L2_cond_mb1': (0.0, 0.1),
     'L2_cond_mb2': (0.0, 0.1),
     'L3_cond_b_down': (0.0, 0.1),
     'L3_cond_b_up': (0.0, 0.1),
     'L3_cond_ln_w': (1.0, 0.2),
     'L3_cond_ln_b': (0.0, 0.1)}
    factors = {'L0_cond_Wq': 3.878, 'L0_cond_Wk': 3.809}
    for name, (base, spread) in spreads.items():
        noise = np.random.default_rng([zlib.crc32(name.encode()), seed]).standard_normal(out[name].shape)
        drawn = base * np.exp(spread * noise) if base else spread * noise
        out[name] = jnp.asarray(drawn.astype(out[name].dtype))
    for name, factor in factors.items():
        out[name] = (out[name] * factor).astype(out[name].dtype)
    return out
```

```python
from contextlib import ExitStack

import concourse.bass as bass
from concourse import mybir


F32 = mybir.dt.float32
F32R = mybir.dt.float32r
I32 = mybir.dt.int32
ALU = mybir.AluOpType
ACT = mybir.ActivationFunctionType
AX_X = mybir.AxisListType.X

P = 128
V = 512
KC = V // P
HID = 4 * V
BN = 256
ROLES = 3
BATCHES, SEQ = 32, 64
HALVES = 2
LAYERS = 2
T = BATCHES * SEQ // HALVES
NB = BATCHES // HALVES
TB = 512
NTB = T // TB
TILES = T // P
TPB = TB // P
GH = 256
MC = GH // P
NG = HID // GH
STEPS = NG * NTB
UP_C, UP_M = KC * GH, 2 * KC * GH
DN = MC * V
LOT = UP_M + DN
JOBS = 2 * NG + 4
RP = BN + 3 * V
SCALE = float(V) ** -0.5
EPS = 1e-5
CB1, MB1 = 0, HID // P
BP, CB2, MB2 = 2 * (HID // P), 2 * (HID // P) + KC, 2 * (HID // P) + 2 * KC
NBIAS = 2 * (HID // P) + 3 * KC

HI, LO = 0, 1
PRODUCTS = ((HI, HI), (HI, LO), (LO, HI))


def cond_seq_kernel(nc, x_in, fuse_in, c_in, m_in, down_in, up_in, roles_in, bias_in, codes_in, role_in, out):
    with ExitStack() as ctx:
        def sb(name, shape, dt):
            return ctx.enter_context(nc.sbuf_tensor(name, shape, dt))

        def sem(name):
            return ctx.enter_context(nc.semaphore(name))

        fused = nc.dram_tensor("fused", (2 * LAYERS, P, KC * V), F32, kind="Internal").ap()
        x = sb("x", [P, KC, T], F32)
        acc = sb("acc", [P, KC * T], F32)
        accv = acc[:, :].rearrange("p (k t) -> p k t", k=KC)
        aT = sb("aT", [P, 2, KC, T], F32R)
        cT = sb("cT", [P, 2, KC * T], F32R)
        cTv = cT[:, :, :].rearrange("p s (k t) -> p s k t", k=KC)
        slot = [sb(f"slot{i}", [P, 2, LOT], F32R) for i in range(2)]
        raw = sb("raw", [P, LOT], F32)
        hraw = sb("hraw", [P, 2, 512], F32)
        hs = sb("hs", [P, 2, 2, 2, 512], F32R)
        hz = sb("hz", [P, 2, 2, 2, 4, SEQ], F32R)
        rolep = sb("rolep", [P, 2, RP], F32)
        ident = sb("ident", [P, P], F32)
        bias = sb("bias", [P, LAYERS, NBIAS], F32)
        codes_i = sb("codes_i", [P, BATCHES], I32)
        codes = sb("codes", [P, BATCHES], F32)
        feat = sb("feat", [P, KC], F32)
        oh = sb("oh", [P, LAYERS, KC, BATCHES], F32)
        roles = sb("roles", [1, BATCHES], I32)
        mx = sb("mx", [P, TPB], F32)
        rsum = sb("rsum", [P, TPB], F32)
        rinv = sb("rinv", [P, TPB], F32)
        stats = sb("stats", [P, 2, 6], F32)
        mv = sb("mv", [P, 2, 2], F32)
        veps = sb("veps", [P, 2, 1], F32)
        rstd = sb("rstd", [P, 2, 1], F32)
        mhalf = sb("mhalf", [P, 1], F32)
        ps = [ctx.enter_context(nc.psum_tensor(f"ps{i}", [P, 512], F32)) for i in range(8)]

        hflat = hraw[:, :, :].rearrange("p a b -> p (a b)")
        pblk = hflat[:, 0:512].rearrange("p (i k) -> p i k", i=TPB)
        sm = hflat[:, 512:768].rearrange("p (i k) -> p i k", i=TPB)
        ex = hflat[:, 768:1024].rearrange("p (i k) -> p i k", i=TPB)

        def tmp(s, a, n):
            return acc[:, s * 2048 + a:s * 2048 + a + n]

        xc = [tmp(s, 0, 512).rearrange("p (k t) -> p k t", k=KC) for s in range(2)]
        yn = [tmp(s, 512, 512) for s in range(2)]
        hp = [tmp(s, 1024, 256) for s in range(2)]
        hg = [tmp(s, 1280, 256) for s in range(2)]
        y = [tmp(s, 1536, 512) for s in range(2)]
        xz = [hs[:, s, :, :, :].rearrange("p l m (k b t) -> p l (m k) b t", k=2, b=4) for s in range(2)]

        consts_in = sem("consts_in")
        x_loaded = [sem(f"x_loaded{b}") for b in range(NTB)]
        fuse_loaded = [sem(f"fuse_loaded{n}") for n in range(2 * LAYERS)]
        fuse_mm, fuse_copied = sem("fuse_mm"), sem("fuse_copied")
        fuse_stored = [sem(f"fuse_stored{s}") for s in range(2)]
        made = sem("made")
        codes_ready, oh_ready = sem("codes_ready"), sem("oh_ready")
        raw_loaded, w_hi, w_lo = sem("raw_loaded"), sem("w_hi"), sem("w_lo")
        xs_hi, xs_lo = sem("xs_hi"), sem("xs_lo")
        t_done, t_hi, t_lo = sem("t_done"), sem("t_hi"), sem("t_lo")
        v_done, v_hi, v_lo = sem("v_done"), sem("v_hi"), sem("v_lo")
        s_done, mx_done, sm_ready, ex_done = sem("s_done"), sem("mx_done"), sem("sm_ready"), sem("ex_done")
        rs_done, ri_done, p_zeroed, p_ready = sem("rs_done"), sem("ri_done"), sem("p_zeroed"), sem("p_ready")
        pt_done, pt_hi, pt_lo = sem("pt_done"), sem("pt_hi"), sem("pt_lo")
        pv_done, a_hi, a_lo = sem("pv_done"), sem("a_hi"), sem("a_lo")
        acc_init = sem("acc_init")
        up_done, h_hi, h_lo, dn_done, acc_done = (sem(n) for n in ("up_done", "h_hi", "h_lo", "dn_done", "acc_done"))
        c_hi, c_lo = sem("c_hi"), sem("c_lo")
        xz_zeroed, xc_done, xz_hi, xz_lo = sem("xz_zeroed"), sem("xc_done"), sem("xz_hi"), sem("xz_lo")
        t1_done, xb_done, d_done, hp_done, hg_done = (sem(n) for n in ("t1_done", "xb_done", "d_done", "hp_done", "hg_done"))
        t2_done, hz_hi, hz_lo, u_done, y_done = (sem(n) for n in ("t2_done", "hz_hi", "hz_lo", "u_done", "y_done"))
        st_done, ag_done, ve_done, rstd_done = (sem(n) for n in ("st_done", "ag_done", "ve_done", "rstd_done"))
        yn_done, g_done, rp_free = sem("yn_done"), sem("g_done"), sem("rp_free")
        rp_loaded = [sem(f"rp_loaded{s}") for s in range(2)]
        t3_done, x_back = sem("t3_done"), sem("x_back")
        stored = [sem(f"stored{s}") for s in range(2)]

        def job_qk(p): return JOBS * p
        def job_vp(p): return JOBS * p + 1
        def job_c(p, g): return JOBS * p + 2 + g
        def job_m(p, g): return JOBS * p + 2 + NG + g
        def job_d(p): return JOBS * p + 2 + 2 * NG
        def job_u(p): return JOBS * p + 3 + 2 * NG

        def fused_w(w, part):
            return cT[:, part, w * 2048:(w + 1) * 2048].rearrange("p (k n) -> p k n", k=KC)

        block = ctx.enter_context(nc.Block())

        @block.sync
        def _(sp):
            sp.dma_start(bias[:, :, :], bias_in).then_inc(consts_in, 16)
            sp.dma_start(codes_i[:, :], codes_in).then_inc(consts_in, 16)
            sp.dma_start(roles[:, :], role_in).then_inc(consts_in, 16)
            rflat = rolep[:, :, :].rearrange("p a b -> p (a b)")
            fuse_at = [(acc[:, 0:2048], acc[:, 2048:4096]), (rflat[:, 0:2048], raw[:, 0:2048])]
            for n in range(2 * LAYERS):
                if n >= 2:
                    sp.wait_ge(fuse_mm, KC * (n - 1))
                for o in range(2):
                    sp.dma_start(fuse_at[n % 2][o], fuse_in[n, o]).then_inc(fuse_loaded[n], 16)
                if n >= 1:
                    for q in range(KC * (n - 1), KC * n):
                        sp.wait_ge(fuse_copied, q + 1)
                        sp.dma_start(fused[q // KC, :, (q % KC) * V:(q % KC + 1) * V], hraw[:, q % 2, :]).then_inc(fuse_stored[q % 2], 16)
            for q in range(KC * (2 * LAYERS - 1), KC * 2 * LAYERS):
                sp.wait_ge(fuse_copied, q + 1)
                sp.dma_start(fused[q // KC, :, (q % KC) * V:(q % KC + 1) * V], hraw[:, q % 2, :]).then_inc(fuse_stored[q % 2], 16)
            for s in range(2):
                sp.wait_ge(fuse_stored[s], 16 * KC * LAYERS)
            sp.dma_start(raw[:, 0:2048], fused[0]).then_inc(raw_loaded, 16)
            sp.wait_ge(w_lo, 1)
            sp.dma_start(raw[:, 0:2048], fused[1]).then_inc(raw_loaded, 16)

            sp.wait_ge(consts_in, 48)

            def load_job(job, src, n):
                sp.wait_ge(w_lo, job)
                sp.dma_start(raw[:, 0:n], src).then_inc(raw_loaded, 16)

            def load_role(p, half, i, s):
                sp.wait_ge(rp_free, 8 * p + i + 1)
                sp.nop(nofuse=True)
                for b in range(2):
                    r = sp.value_load(roles[0:1, bass.ds(half * NB + 2 * i + b, 1)], min_val=0, max_val=ROLES - 1)
                    src = roles_in[p_layer[0], bass.ds(r, 1), :].to_broadcast([SEQ, RP])
                    sp.dma_start(rolep[b * SEQ:(b + 1) * SEQ, s, :], src).then_inc(rp_loaded[s], 16)

            def store(p, half, i, s):
                sp.wait_ge(rp_free, 8 * p + i + 3)
                sp.dma_start(out[bass.ds(half * T + i * P, P), :], yn[s]).then_inc(stored[s], 16)

            p_layer = [0]
            with sp.Fori(0, HALVES) as half:
                sp.wait_ge(xc_done, 2 * TILES * half + 1)
                for b in range(NTB):
                    sp.dma_start(x[:, :, b * TB:(b + 1) * TB], x_in[bass.ds(half, 1), b].rearrange("o p k t -> p (o k) t")).then_inc(x_loaded[b], 16)
                for layer in range(LAYERS):
                    p_layer[0] = layer
                    p = 2 * half + layer
                    load_job(job_c(p, 0), c_in[layer, 0], UP_C + DN)
                    load_role(p, half, 0, 0)
                    load_role(p, half, 1, 1)
                    with sp.Fori(1, NG) as g:
                        load_job(job_c(p, g), c_in[layer, bass.ds(g, 1)].rearrange("o p n -> p (o n)"), UP_C + DN)
                    with sp.Fori(0, NG) as g:
                        load_job(job_m(p, g), m_in[layer, bass.ds(g, 1)].rearrange("o p n -> p (o n)"), LOT)
                    load_job(job_d(p), down_in[layer], LOT)
                    load_job(job_u(p), up_in[layer], LOT)
                    nxt = 2 * ((layer + 1) % LAYERS)
                    load_job(job_qk(p + 1), fused[nxt], 2048)
                    load_job(job_vp(p + 1), fused[nxt + 1], 2048)
                    with sp.Fori(0, TILES // 2 - 1) as pair:
                        for s in range(2):
                            if layer == 1:
                                store(p, half, 2 * pair + s, s)
                            load_role(p, half, 2 * pair + 2 + s, s)
                    if layer == 1:
                        for s in range(2):
                            store(p, half, TILES - 2 + s, s)
            for s in range(2):
                sp.wait_ge(stored[s], 16 * HALVES * TILES // 2)

        @block.gpsimd
        def _(pool):
            nc.gpsimd.memset(ident[:, :], 0.0).then_inc(made, 1)
            nc.gpsimd.iota(feat[:, :], [[P, KC]], base=0, channel_multiplier=1,
                           allow_small_or_imprecise_dtypes=True).then_inc(made, 1)
            nc.gpsimd.memset(mhalf[:, :], -0.5).then_inc(made, 1)
            pool.wait_ge(made, 1)
            nc.gpsimd.affine_select(out=ident[:, :], in_=ident[:, :], compare_op=ALU.not_equal, fill=1.0,
                                    base=0, pattern=[[-1, P]], channel_multiplier=1).then_inc(made, 1)
            for s in range(2):
                nc.gpsimd.memset(hz[:, s, :, :, 1, :].bitcast(F32), 0.0).then_inc(rp_free, 1)

            with pool.Fori(0, HALVES) as half:
                for layer in range(LAYERS):
                    p = 2 * half + layer
                    pool.wait_ge(xs_lo, 2 * KC * p + 1)
                    pool.wait_ge(oh_ready, LAYERS * KC)
                    pool.nop(nofuse=True)
                    nc.gpsimd.memset(pblk, 0.0).then_inc(p_zeroed, 1)
                    for k in range(KC):
                        nc.gpsimd.tensor_copy(accv[:, k, :].rearrange("p (b t) -> p b t", b=NB),
                                              oh[:, layer, k, bass.ds(half * NB, NB)].unsqueeze(2).to_broadcast([P, NB, SEQ])
                                              ).then_inc(acc_init, 1)
                    for s in range(2):
                        pool.wait_ge(dn_done, 128 * p + 124 + 4 * s)
                        pool.nop(nofuse=True)
                        nc.gpsimd.memset(hs[:, s, :, :, :].rearrange("p l m (k b t) -> p (l m k) b t", k=2, b=4)[:, :, 1, :].bitcast(F32), 0.0).then_inc(xz_zeroed, 1)
                    with pool.Fori(0, TILES // 2) as pair:
                        for s in range(2):
                            e = 8 * p + 2 * pair + s
                            pool.wait_ge(ve_done, e + 1)
                            nc.gpsimd.tensor_tensor(rstd[:, s, :], veps[:, s, :], mhalf[:, :], ALU.pow).then_inc(rstd_done, 1)
                            pool.wait_ge(yn_done, e + 1)
                            nc.gpsimd.tensor_tensor(yn[s], yn[s], rolep[:, s, BN + V:BN + 2 * V], ALU.mult).then_inc(g_done, 1)
                            pool.wait_ge(g_done, e + 1)
                            nc.gpsimd.tensor_tensor(yn[s], yn[s], rolep[:, s, BN + 2 * V:BN + 3 * V], ALU.add).then_inc(rp_free, 1)
                    if layer == 1:
                        for s in range(2):
                            pool.wait_ge(stored[s], 16 * (TILES // 2) * (half + 1))

        @block.tensor
        def _(pe):
            pe.wait_ge(made, 4)
            rflat = rolep[:, :, :].rearrange("p a b -> p (a b)")
            fuse_at = [(acc[:, 0:2048], acc[:, 2048:4096]), (rflat[:, 0:2048], raw[:, 0:2048])]
            for n in range(2 * LAYERS):
                pe.wait_ge(fuse_loaded[n], 32)
                a, b = fuse_at[n % 2]
                for c in range(KC):
                    if n >= 2:
                        pe.wait_ge(fuse_copied, KC * (n - 2) + c + 1)
                    for k in range(KC):
                        mm = nc.tensor.matmul(ps[4 * (n % 2) + c][:, :], a[:, k * V + c * P:k * V + (c + 1) * P],
                                              b[:, k * V:(k + 1) * V], start=(k == 0), stop=(k == KC - 1))
                    mm.then_inc(fuse_mm, 1)
            pe.wait_ge(fuse_copied, KC * 2 * LAYERS)
            pe.wait_ge(consts_in, 48)

            def product(out, pairs, start=True, stop=True):
                n, total = 0, 3 * len(pairs)
                for lhs, rhs, wait in pairs:
                    if wait is not None:
                        pe.wait_ge(*wait)
                    for a, b in PRODUCTS:
                        mm = nc.tensor.matmul(out, lhs(a), rhs(b), start=(start and n == 0), stop=(stop and n == total - 1))
                        n += 1
                return mm

            def attention(p, b):
                cols = slice(b * TB, (b + 1) * TB)
                if b == 0:
                    pe.wait_ge(w_lo, job_qk(p) + 1)
                else:
                    pe.wait_ge(a_lo, 8 * p + KC)
                for j in range(KC):
                    product(ps[2 + j][:, :], [
                        (lambda a, k=k: fused_w(0, a)[:, k, j * P:(j + 1) * P], lambda c, k=k: aT[:, c, k, cols],
                         (xs_lo, 8 * p + KC * b + k + 1) if j == 0 else None) for k in range(KC)]).then_inc(t_done, 1)
                if b == 0:
                    pe.wait_ge(w_lo, job_vp(p) + 1)

                def values(i):
                    n = 8 * p + TPB * b + i
                    if b or i >= 2:
                        pe.wait_ge(v_lo, n - 1)
                    product(ps[i % 2][:, :], [
                        (lambda a, k=k: aT[:, a, k, b * TB + i * P:b * TB + (i + 1) * P], lambda c, k=k: fused_w(1, c)[:, k, :], None)
                        for k in range(KC)]).then_inc(v_done, 1)

                def scores():
                    for i in range(TPB):
                        mm = product(ps[6][:, i * P:(i + 1) * P], [
                            (lambda a, j=j: hs[:, j // 2, a, j % 2, i * P:(i + 1) * P],
                             lambda c, j=j: aT[:, c, j, b * TB + i * P:b * TB + (i + 1) * P],
                             (t_lo, 8 * p + KC * b + j + 1) if i == 0 else None) for j in range(KC)])
                    mm.then_inc(s_done, 1)

                values(0)
                scores()
                values(1)
                values(2)
                pe.wait_ge(p_ready, 4 * p + 2 * b + 2)
                for i in range(TPB):
                    mm = nc.tensor.transpose(ps[7][:, i * P:(i + 1) * P], pblk[:, i, :], ident[:, :])
                mm.then_inc(pt_done, 1)
                values(3)
                pe.wait_ge(pt_lo, 2 * p + b + 1)
                pe.wait_ge(v_lo, 8 * p + TPB * b + TPB)
                for f in range(KC):
                    for i in range(TPB):
                        mm = product(ps[2 + f][:, i * P:(i + 1) * P], [
                            (lambda a: slot[1][:, a, i * V + f * P:i * V + (f + 1) * P],
                             lambda c: slot[1][:, c, 2048 + i * P:2048 + (i + 1) * P], None)])
                    mm.then_inc(pv_done, 1)

            def up(p, r, kind, g_job, s, b):
                kin = KC * (1 + kind)
                if b == 0:
                    pe.wait_ge(w_lo, g_job + 1)
                for m in range(MC):
                    if not (kind == 0 and isinstance(r, int) and r == 0):
                        pe.wait_ge(h_hi, 64 * p + 2 * (r - 1) + m + 1)
                    pairs = []
                    for k in range(kin):
                        src = aT if k < KC else cTv
                        wait = None
                        if m == 0 and kind == 0 and k == 0:
                            wait = (a_lo, 8 * p + KC * (b + 1))
                        if m == 0 and kind == 1 and k >= KC:
                            wait = (c_lo, 8 * p + KC * b + k - KC + 1)
                        pairs.append((lambda a, k=k: slot[s][:, a, k * GH + m * P:k * GH + (m + 1) * P],
                                      lambda c, k=k, src=src: src[:, c, k % KC, b * TB:(b + 1) * TB], wait))
                    product(ps[m][:, :], pairs).then_inc(up_done, 1)

            def down(p, r, kind, s, b):
                base = UP_M if kind else UP_C
                for o in range(KC):
                    if not (kind == 0 and isinstance(r, int) and r == 0):
                        pe.wait_ge(acc_done, 128 * p + 4 * (r - 1) + o + 1)
                    product(ps[2 + o][:, :], [
                        (lambda a, m=m: slot[s][:, a, base + m * V + o * P:base + m * V + (o + 1) * P],
                         lambda c, m=m: hs[:, b, c, m, :],
                         (h_lo, 64 * p + 2 * r + m + 1) if o == 0 else None) for m in range(MC)]).then_inc(dn_done, 1)

            def mlp(p, kind):
                job = job_m if kind else job_c
                first = STEPS * kind
                up(p, first, kind, job(p, 0), 0, 0)

                def four(g0, last):
                    for t in range(4):
                        r = first + 2 * g0 + t
                        if not (last and t == 3):
                            n = t + 1
                            up(p, r + 1, kind, job(p, g0 + n // 2), (n // 2) % 2, n % 2)
                        down(p, r, kind, (t // 2) % 2, t % 2)

                if kind == 0:
                    four(0, False)
                    with pe.Fori(1, NG // 2 - 1) as gp:
                        four(2 * gp, False)
                else:
                    with pe.Fori(0, NG // 2 - 1) as gp:
                        four(2 * gp, False)
                four(NG - 2, True)

            def tile_roles(half, i):
                pe.nop(nofuse=True)
                return [pe.value_load(roles[0:1, bass.ds(half * NB + 2 * i + b, 1)], min_val=0, max_val=ROLES - 1)
                        for b in range(2)]

            def front(p, half, i, s):
                e = 8 * p + i
                r = tile_roles(half, i)
                pe.wait_ge(xc_done, e + 2)
                if not (isinstance(i, int) and i < 2):
                    pe.wait_ge(xb_done, e - 1)
                for k in range(KC):
                    mm = nc.tensor.transpose(ps[5 * s][:, k * P:(k + 1) * P], xc[s][:, k, :], ident[:, :])
                mm.then_inc(t1_done, 1)
                if isinstance(i, int) and i == 0:
                    pe.wait_ge(w_lo, job_d(p) + 1)
                    pe.wait_ge(xz_zeroed, 2 * p + 2)
                if not (isinstance(i, int) and i < 2):
                    pe.wait_ge(hp_done, e - 1)
                pe.wait_ge(xz_lo, e + 1)
                bank = ps[1 + 6 * s][:, 0:BN]
                n = 0
                for b in range(2):
                    for k in range(KC):
                        for a, c in PRODUCTS:
                            lhs = xz[s][:, a, k, b:b + 2, :]
                            mm = nc.tensor.matmul(bank, lhs, slot[0][:, c, bass.ds(r[b] * (KC * BN) + k * BN, BN)],
                                                  start=(n == 0), stop=(n == 6 * KC - 1))
                            n += 1
                mm.then_inc(d_done, 1)

            def turn_h(p, i, s):
                e = 8 * p + i
                pe.wait_ge(hg_done, e + 1)
                if not (isinstance(i, int) and i == 0):
                    pe.wait_ge(hz_lo, e)
                for k in range(2):
                    mm = nc.tensor.transpose(ps[2][:, k * P:(k + 1) * P], hg[s][:, k * P:(k + 1) * P], ident[:, :])
                mm.then_inc(t2_done, 1)

            def adapter_up(p, half, i, s):
                e = 8 * p + i
                r = tile_roles(half, i)
                if isinstance(i, int) and i == 0:
                    pe.wait_ge(w_lo, job_u(p) + 1)
                if not (isinstance(i, int) and i < 2):
                    pe.wait_ge(y_done, e - 1)
                pe.wait_ge(hz_lo, e + 1)
                n = 0
                for b in range(2):
                    for k in range(2):
                        for a, c in PRODUCTS:
                            mm = nc.tensor.matmul(ps[3 + 3 * s][:, :], hz[:, s, a, k, b:b + 2, :],
                                                  slot[1][:, c, bass.ds(r[b] * (2 * V) + k * V, V)],
                                                  start=(n == 0), stop=(n == 11))
                            n += 1
                mm.then_inc(u_done, 1)

            def turn_back(p, half, layer, i, s):
                if layer == 1:
                    return
                pe.wait_ge(rp_free, 8 * p + i + 3)
                if not (isinstance(i, int) and i == 0):
                    pe.wait_ge(x_back, 8 * half + i)
                for k in range(KC):
                    mm = nc.tensor.transpose(ps[4][:, k * P:(k + 1) * P], yn[s][:, k * P:(k + 1) * P], ident[:, :])
                mm.then_inc(t3_done, 1)

            with pe.Fori(0, HALVES) as half:
                for layer in range(LAYERS):
                    p = 2 * half + layer
                    for b in range(NTB):
                        attention(p, b)
                    mlp(p, 0)
                    mlp(p, 1)
                    pe.wait_ge(acc_done, 128 * p + 128)

                    def step(i, s):
                        peeled = isinstance(i, int)
                        if not (peeled and i == TILES - 1):
                            front(p, half, i + 1, 1 - s)
                        adapter_up(p, half, i, s)
                        if not (peeled and i == 0):
                            turn_back(p, half, layer, i - 1, 1 - s)
                        if not (peeled and i == TILES - 1):
                            turn_h(p, i + 1, 1 - s)

                    front(p, half, 0, 0)
                    turn_h(p, 0, 0)
                    step(0, 0)
                    step(1, 1)
                    with pe.Fori(1, TILES // 2 - 1) as pair:
                        step(2 * pair, 0)
                        step(2 * pair + 1, 1)
                    step(TILES - 2, 0)
                    step(TILES - 1, 1)
                    turn_back(p, half, layer, TILES - 1, 1)
                    if layer == 0:
                        pe.wait_ge(x_back, 8 * (half + 1))
                    pe.wait_ge(y_done, 8 * p + 8)

        @block.scalar
        def _(act):
            def split_hi(job, n, dst, *free):
                act.wait_ge(raw_loaded, 16 * (job + 1))
                for w in free:
                    act.wait_ge(*w)
                nc.scalar.activation(dst, raw[:, 0:n], ACT.Copy).then_inc(w_hi, 1)

            split_hi(0, 2048, cT[:, HI, 0:2048])
            split_hi(1, 2048, cT[:, HI, 2048:4096])
            act.wait_ge(consts_in, 48)

            def attention(p, half, layer, b):
                cols = slice(b * TB, (b + 1) * TB)
                if layer == 0:
                    act.wait_ge(x_loaded[b], 16 * (half + 1))
                else:
                    act.wait_ge(x_back, 8 * (half + 1))
                for k in range(KC):
                    nc.scalar.activation(aT[:, HI, k, cols], x[:, k, cols], ACT.Copy).then_inc(xs_hi, 1)
                for j in range(KC):
                    act.wait_ge(t_done, 8 * p + KC * b + j + 1)
                    nc.scalar.activation(hs[:, j // 2, HI, j % 2, :], ps[2 + j][:, :], ACT.Copy).then_inc(t_hi, 1)

                def values(i):
                    act.wait_ge(v_done, 8 * p + TPB * b + i + 1)
                    nc.scalar.activation(slot[1][:, HI, i * V:(i + 1) * V], ps[i % 2][:, :], ACT.Copy).then_inc(v_hi, 1)

                values(0)
                act.wait_ge(sm_ready, 4 * p + 2 * b + 2)
                nc.scalar.activation(ex, sm, ACT.Exp, scale=SCALE).then_inc(ex_done, 1)
                values(1)
                values(2)
                act.wait_ge(pt_done, 2 * p + b + 1)
                nc.scalar.activation(slot[1][:, HI, 2048:2560], ps[7][:, :], ACT.Copy).then_inc(pt_hi, 1)
                values(3)
                if b == 0:
                    split_hi(job_c(p, 0), UP_C + DN, slot[0][:, HI, 0:UP_C + DN])
                for f in range(KC):
                    act.wait_ge(pv_done, 8 * p + KC * b + f + 1)
                    nc.scalar.activation(aT[:, HI, f, cols], ps[2 + f][:, :], ACT.Identity,
                                         bias=bias[:, layer, BP + f:BP + f + 1]).then_inc(a_hi, 1)

            def hidden(p, layer, kind, r, g, b):
                for m in range(MC):
                    act.wait_ge(up_done, 64 * p + 2 * r + m + 1)
                    early = kind == 0 and isinstance(r, int)
                    if not (early and r == 0):
                        act.wait_ge(h_lo, 64 * p + 2 * (r - 1) + m + 1)
                    if not (early and r < 2):
                        act.wait_ge(dn_done, 128 * p + 4 * (r - 1))
                    col = (MB1 if kind else CB1) + MC * g + m
                    b1 = bias[:, layer, bass.ds(col, 1)]
                    act.nop(nofuse=True)
                    nc.scalar.activation(hraw[:, m, :], ps[m][:, :], ACT.Gelu, bias=b1)
                    nc.scalar.activation(hs[:, b, HI, m, :], ps[m][:, :], ACT.Gelu, bias=b1).then_inc(h_hi, 1)

            def mlp(p, layer, kind):
                n = LOT if kind else UP_C + DN
                job = job_m if kind else job_c
                first = STEPS * kind

                def group(g, s, nxt, first_c=False):
                    r = first + 2 * g
                    hidden(p, layer, kind, r, g, 0)
                    if nxt:
                        free = (pv_done, 8 * p + 8) if first_c else (dn_done, 128 * p + 4 * r)
                        split_hi(job(p, g + 1), n, slot[1 - s][:, HI, 0:n], free)
                    elif kind == 0:
                        split_hi(job_m(p, 0), LOT, slot[0][:, HI, 0:LOT], (dn_done, 128 * p + 4 * r))
                    else:
                        split_hi(job_d(p), LOT, slot[0][:, HI, 0:LOT], (dn_done, 128 * p + 4 * r))
                    hidden(p, layer, kind, r + 1, g, 1)

                if kind == 0:
                    group(0, 0, True, True)
                    group(1, 1, True)
                    with act.Fori(1, NG // 2 - 1) as gp:
                        group(2 * gp, 0, True)
                        group(2 * gp + 1, 1, True)
                else:
                    with act.Fori(0, NG // 2 - 1) as gp:
                        group(2 * gp, 0, True)
                        group(2 * gp + 1, 1, True)
                group(NG - 2, 0, True)
                group(NG - 1, 1, False)

            with act.Fori(0, HALVES) as half:
                for layer in range(LAYERS):
                    p = 2 * half + layer
                    for b in range(NTB):
                        attention(p, half, layer, b)
                    mlp(p, layer, 0)
                    for b in range(NTB):
                        for o in range(KC):
                            act.wait_ge(acc_done, 128 * p + 4 * (STEPS - 2 + b) + o + 1)
                            nc.scalar.activation(cTv[:, HI, o, b * TB:(b + 1) * TB], accv[:, o, b * TB:(b + 1) * TB],
                                                 ACT.Copy).then_inc(c_hi, 1)
                    mlp(p, layer, 1)

                    def split_x(i, s):
                        e = 8 * p + i
                        act.wait_ge(xc_done, e + 2)
                        if isinstance(i, int) and i < 2:
                            act.wait_ge(dn_done, 128 * p + 124 + 4 * i)
                        else:
                            act.wait_ge(d_done, e - 1)
                        nc.scalar.activation(xz[s][:, HI, :, 0:3:2, :], xc[s].rearrange("p k (b t) -> p k b t", b=2),
                                             ACT.Copy).then_inc(xz_hi, 1)

                    def gelu_h(i, s):
                        act.wait_ge(hp_done, 8 * p + i + 1)
                        nc.scalar.activation(hg[s], hp[s], ACT.Gelu).then_inc(hg_done, 1)

                    def split_h(i, s):
                        act.wait_ge(t2_done, 8 * p + i + 1)
                        nc.scalar.activation(hz[:, s, HI, :, 0:3:2, :], ps[2][:, 0:BN].rearrange("p (k b t) -> p k b t", k=2, b=2),
                                             ACT.Copy).then_inc(hz_hi, 1)

                    def back(i, s):
                        if layer == 1:
                            return
                        act.wait_ge(t3_done, 8 * half + i + 1)
                        nc.scalar.activation(x[:, :, bass.ds(i * P, P)], ps[4][:, :].rearrange("p (k t) -> p k t", k=KC),
                                             ACT.Copy).then_inc(x_back, 1)

                    def step(i, s):
                        peeled = isinstance(i, int)
                        split_h(i, s)
                        if not (peeled and i >= TILES - 2):
                            split_x(i + 2, s)
                        if not (peeled and i == TILES - 1):
                            gelu_h(i + 1, 1 - s)
                        if not (peeled and i == 0):
                            back(i - 1, 1 - s)

                    split_x(0, 0)
                    split_x(1, 1)
                    split_hi(job_u(p), LOT, slot[1][:, HI, 0:LOT], (dn_done, 128 * p + 128))
                    gelu_h(0, 0)
                    step(0, 0)
                    split_hi(job_qk(p + 1), 2048, cT[:, HI, 0:2048])
                    step(1, 1)
                    with act.Fori(1, TILES // 2 - 1) as pair:
                        step(2 * pair, 0)
                        step(2 * pair + 1, 1)
                    step(TILES - 2, 0)
                    step(TILES - 1, 1)
                    split_hi(job_vp(p + 1), 2048, cT[:, HI, 2048:4096])
                    back(TILES - 1, 1)

        @block.vector
        def _(dve):
            def minus(out, a, hi):
                return nc.vector.tensor_tensor(out, a, hi.bitcast(F32), ALU.subtract)

            def split_lo(job, n, dst):
                dve.wait_ge(w_hi, job + 1)
                minus(dst[:, LO, :], raw[:, 0:n], dst[:, HI, :]).then_inc(w_lo, 1)

            dve.wait_ge(consts_in, 48)
            nc.vector.tensor_copy(codes[:, :], codes_i[:, :]).then_inc(codes_ready, 1)
            dve.wait_ge(codes_ready, 1)
            dve.wait_ge(made, 4)
            for layer in range(LAYERS):
                for k in range(KC):
                    nc.vector.tensor_scalar(oh[:, layer, k, :], codes[:, :], feat[:, k:k + 1],
                                            bias[:, layer, CB2 + k:CB2 + k + 1], ALU.is_equal, ALU.add).then_inc(oh_ready, 1)
            nc.vector.memset(mx[:, :], 0.0).then_inc(xc_done, 1)
            for q in range(KC * 2 * LAYERS):
                dve.wait_ge(fuse_mm, q + 1)
                if q >= 2:
                    dve.wait_ge(fuse_stored[q % 2], 16 * (q // 2))
                nc.vector.tensor_copy(hraw[:, q % 2, :], ps[4 * (q // KC % 2) + q % KC][:, :]).then_inc(fuse_copied, 1)
            split_lo(0, 2048, cT[:, :, 0:2048])
            split_lo(1, 2048, cT[:, :, 2048:4096])

            def attention(p, layer, b):
                cols = slice(b * TB, (b + 1) * TB)
                for k in range(KC):
                    dve.wait_ge(xs_hi, 8 * p + KC * b + k + 1)
                    minus(aT[:, LO, k, cols], x[:, k, cols], aT[:, HI, k, cols]).then_inc(xs_lo, 1)
                for j in range(KC):
                    dve.wait_ge(t_hi, 8 * p + KC * b + j + 1)
                    minus(hs[:, j // 2, LO, j % 2, :], ps[2 + j][:, :], hs[:, j // 2, HI, j % 2, :]).then_inc(t_lo, 1)

                def values(i):
                    dve.wait_ge(v_hi, 8 * p + TPB * b + i + 1)
                    minus(slot[1][:, LO, i * V:(i + 1) * V], ps[i % 2][:, :], slot[1][:, HI, i * V:(i + 1) * V]).then_inc(v_lo, 1)

                values(0)
                diag = [ps[6][h * SEQ:(h + 1) * SEQ, :].rearrange("p (i h k) -> p i h k", i=TPB, h=2)[:, :, h, :] for h in range(2)]
                rows = [slice(h * SEQ, (h + 1) * SEQ) for h in range(2)]
                dve.wait_ge(s_done, 2 * p + b + 1)
                for h in range(2):
                    nc.vector.tensor_reduce(mx[rows[h], :], diag[h], AX_X, ALU.max).then_inc(mx_done, 1)
                for h in range(2):
                    dve.wait_ge(mx_done, 4 * p + 2 * b + h + 1)
                    nc.vector.tensor_tensor(sm[rows[h], :, :], diag[h], mx[rows[h], :].unsqueeze(2).to_broadcast([SEQ, TPB, SEQ]),
                                            ALU.subtract).then_inc(sm_ready, 1)
                dve.wait_ge(ex_done, 2 * p + b + 1)
                nc.vector.tensor_reduce(rsum[:, :], ex, AX_X, ALU.add).then_inc(rs_done, 1)
                dve.wait_ge(rs_done, 2 * p + b + 1)
                nc.vector.reciprocal(rinv[:, :], rsum[:, :]).then_inc(ri_done, 1)
                dve.wait_ge(ri_done, 2 * p + b + 1)
                dve.wait_ge(p_zeroed, p + 1)
                for h in range(2):
                    nc.vector.tensor_tensor(pblk[rows[h], :, h * SEQ:(h + 1) * SEQ], ex[rows[h], :, :],
                                            rinv[rows[h], :].unsqueeze(2).to_broadcast([SEQ, TPB, SEQ]), ALU.mult).then_inc(p_ready, 1)
                values(1)
                values(2)
                dve.wait_ge(pt_hi, 2 * p + b + 1)
                minus(slot[1][:, LO, 2048:2560], ps[7][:, :], slot[1][:, HI, 2048:2560]).then_inc(pt_lo, 1)
                values(3)
                if b == 0:
                    split_lo(job_c(p, 0), UP_C + DN, slot[0][:, :, 0:UP_C + DN])
                for f in range(KC):
                    dve.wait_ge(a_hi, 8 * p + KC * b + f + 1)
                    nc.vector.scalar_tensor_tensor(out=aT[:, LO, f, cols], in0=ps[2 + f][:, :], scalar=bias[:, layer, BP + f:BP + f + 1],
                                                   in1=aT[:, HI, f, cols].bitcast(F32), op0=ALU.add, op1=ALU.subtract).then_inc(a_lo, 1)

            def hidden(p, r, b):
                for m in range(MC):
                    dve.wait_ge(h_hi, 64 * p + 2 * r + m + 1)
                    minus(hs[:, b, LO, m, :], hraw[:, m, :], hs[:, b, HI, m, :]).then_inc(h_lo, 1)

            def add(p, kind, r, b):
                for o in range(KC):
                    dve.wait_ge(dn_done, 128 * p + 4 * r + o + 1)
                    dst = (x[:, o, :] if kind else accv[:, o, :])[:, b * TB:(b + 1) * TB]
                    nc.vector.tensor_tensor(dst, ps[2 + o][:, :], dst, ALU.add).then_inc(acc_done, 1)

            def mlp(p, kind):
                n = LOT if kind else UP_C + DN
                job = job_m if kind else job_c
                first = STEPS * kind
                hidden(p, first, 0)

                def group(g, s, nxt):
                    r = first + 2 * g
                    if nxt:
                        split_lo(job(p, g + 1), n, slot[1 - s][:, :, 0:n])
                    elif kind == 0:
                        split_lo(job_m(p, 0), LOT, slot[0][:, :, 0:LOT])
                    else:
                        split_lo(job_d(p), LOT, slot[0][:, :, 0:LOT])
                    hidden(p, r + 1, 1)
                    add(p, kind, r, 0)
                    if nxt:
                        hidden(p, r + 2, 0)
                        add(p, kind, r + 1, 1)

                with dve.Fori(0, NG // 2 - 1) as gp:
                    group(2 * gp, 0, True)
                    group(2 * gp + 1, 1, True)
                group(NG - 2, 0, True)
                group(NG - 1, 1, False)

            with dve.Fori(0, HALVES) as half:
                for layer in range(LAYERS):
                    p = 2 * half + layer
                    for b in range(NTB):
                        attention(p, layer, b)
                    dve.wait_ge(acc_init, KC * (p + 1))
                    mlp(p, 0)
                    for b in range(NTB):
                        cols = slice(b * TB, (b + 1) * TB)
                        if b == 1:
                            add(p, 0, STEPS - 1, 1)
                        for o in range(KC):
                            dve.wait_ge(acc_done, 128 * p + 4 * (STEPS - 2 + b) + o + 1)
                            nc.vector.scalar_tensor_tensor(out=x[:, o, cols], in0=accv[:, o, cols], scalar=bias[:, layer, MB2 + o:MB2 + o + 1],
                                                           in1=x[:, o, cols], op0=ALU.add, op1=ALU.add)
                            dve.wait_ge(c_hi, 8 * p + KC * b + o + 1)
                            minus(cTv[:, LO, o, cols], accv[:, o, cols], cTv[:, HI, o, cols]).then_inc(c_lo, 1)
                    mlp(p, 1)
                    add(p, 1, 2 * STEPS - 1, 1)
                    dve.wait_ge(acc_done, 128 * p + 128)

                    def clip(i, s):
                        e = 8 * p + i
                        if not (isinstance(i, int) and i < 2):
                            dve.wait_ge(t1_done, e - 1)
                        nc.vector.tensor_scalar(xc[s], x[:, :, bass.ds(i * P, P)], 0.0, 1.0, ALU.max, ALU.min).then_inc(xc_done, 1)

                    def split_x(i, s):
                        dve.wait_ge(xz_hi, 8 * p + i + 1)
                        minus(xz[s][:, LO, :, 0:3:2, :], xc[s].rearrange("p k (b t) -> p k b t", b=2), xz[s][:, HI, :, 0:3:2, :]).then_inc(xz_lo, 1)

                    def x_bias(i, s):
                        e = 8 * p + i
                        dve.wait_ge(t1_done, e + 1)
                        dve.wait_ge(rp_loaded[s], 32 * (4 * p + (i - s) // 2 + 1) if isinstance(i, int) else 16 * (8 * p + (i - s) + 2))
                        if not (isinstance(i, int) and i < 2):
                            if layer == 0:
                                dve.wait_ge(t3_done, 8 * half + i - 1)
                            else:
                                dve.wait_ge(stored[s], 8 * (8 * half + (i - s)))
                        nc.vector.tensor_tensor(yn[s], ps[5 * s][:, :], rolep[:, s, BN:BN + V], ALU.add).then_inc(xb_done, 1)

                    def h_bias(i, s):
                        dve.wait_ge(d_done, 8 * p + i + 1)
                        nc.vector.tensor_tensor(hp[s], ps[1 + 6 * s][:, 0:BN], rolep[:, s, 0:BN], ALU.add).then_inc(hp_done, 1)

                    def split_h(i, s):
                        dve.wait_ge(hz_hi, 8 * p + i + 1)
                        minus(hz[:, s, LO, :, 0:3:2, :], ps[2][:, 0:BN].rearrange("p (k b t) -> p k b t", k=2, b=2),
                              hz[:, s, HI, :, 0:3:2, :]).then_inc(hz_lo, 1)

                    def row_stats(i, s):
                        e = 8 * p + i
                        dve.wait_ge(u_done, e + 1)
                        dve.wait_ge(xb_done, e + 1)
                        nc.vector.tensor_tensor(y[s], ps[3 + 3 * s][:, :], yn[s], ALU.add).then_inc(y_done, 1)
                        dve.wait_ge(y_done, e + 1)
                        nc.vector.bn_stats(stats[:, s, :], y[s]).then_inc(st_done, 1)
                        dve.wait_ge(st_done, e + 1)
                        dve.nop(nofuse=True)
                        nc.vector.bn_aggr(mv[:, s, :], stats[:, s, :]).then_inc(ag_done, 1)
                        dve.wait_ge(ag_done, e + 1)
                        nc.vector.tensor_scalar(veps[:, s, :], mv[:, s, 1:2], EPS, None, ALU.add).then_inc(ve_done, 1)

                    def normalise(i, s):
                        dve.wait_ge(rstd_done, 8 * p + i + 1)
                        nc.vector.tensor_scalar(yn[s], y[s], mv[:, s, 0:1], rstd[:, s, :], ALU.subtract, ALU.mult).then_inc(yn_done, 1)

                    def step(i, s):
                        peeled = isinstance(i, int)
                        split_h(i, s)
                        if not (peeled and i >= TILES - 2):
                            clip(i + 2, s)
                        if not (peeled and i == TILES - 1):
                            x_bias(i + 1, 1 - s)
                        if not (peeled and i >= TILES - 2):
                            split_x(i + 2, s)
                        if not (peeled and i == TILES - 1):
                            h_bias(i + 1, 1 - s)
                        row_stats(i, s)
                        normalise(i, s)

                    clip(0, 0)
                    clip(1, 1)
                    split_x(0, 0)
                    split_x(1, 1)
                    x_bias(0, 0)
                    h_bias(0, 0)
                    split_lo(job_u(p), LOT, slot[1][:, :, 0:LOT])
                    step(0, 0)
                    split_lo(job_qk(p + 1), 2048, cT[:, :, 0:2048])
                    step(1, 1)
                    with dve.Fori(1, TILES // 2 - 1) as pair:
                        step(2 * pair, 0)
                        step(2 * pair + 1, 1)
                    step(TILES - 2, 0)
                    step(TILES - 1, 1)
                    split_lo(job_vp(p + 1), 2048, cT[:, :, 2048:4096])


def _chunks(w):
    import numpy as np
    r, n = w.shape
    return np.ascontiguousarray(w.reshape(r // P, P, n).transpose(1, 0, 2).reshape(P, -1))


def kernel(**inputs):
    import numpy as np
    import concourse.bacc as bacc
    from concourse.bass_utils import run_bass_kernel_spmd

    a = {k: np.asarray(v) for k, v in inputs.items()}
    blocks, adapters = ("L0_cond_", "L2_cond_"), ("L1_cond_", "L3_cond_")
    gains = (("gamma", "beta"), ("ln_w", "ln_b"))

    def groups(w1, w2):
        return np.stack([np.concatenate([_chunks(w1[:, g * GH:(g + 1) * GH]), _chunks(w2[g * GH:(g + 1) * GH])], 1)
                         for g in range(NG)])

    def columns(b):
        return b.reshape(-1, P).T

    arrays = {
        "x_in": np.ascontiguousarray(a["x"].reshape(HALVES, NTB, TB, KC, P).transpose(0, 1, 4, 3, 2)),
        "fuse_in": np.stack([np.stack([_chunks(u), _chunks(w)]) for l in blocks
                             for u, w in ((a[l + "Wq"].T, a[l + "Wk"].T), (a[l + "Wv"].T, a[l + "Wp"]))]),
        "c_in": np.stack([groups(a[l + "cW1"], a[l + "cW2"]) for l in blocks]),
        "m_in": np.stack([groups(a[l + "mW1"], a[l + "mW2"]) for l in blocks]),
        "down_in": np.stack([np.concatenate([_chunks(a[l + "W_down"][r]) for r in range(ROLES)], 1) for l in adapters]),
        "up_in": np.stack([np.concatenate([_chunks(a[l + "W_up"][r]) for r in range(ROLES)], 1) for l in adapters]),
        "roles_in": np.stack([np.concatenate([a[l + "b_down"], a[l + "b_up"], a[l + g], a[l + b]], 1)
                              for l, (g, b) in zip(adapters, gains)]),
        "bias_in": np.ascontiguousarray(np.stack([np.concatenate([columns(a[l + n]) for n in ("cb1", "mb1", "bp", "cb2", "mb2")], 1)
                                                  for l in blocks], 1)),
        "codes_in": np.ascontiguousarray(np.broadcast_to(a["itok_B_17_1546"].reshape(1, BATCHES), (P, BATCHES))),
        "role_in": np.ascontiguousarray(a["itok_B_1_2"].reshape(1, BATCHES)),
    }
    nc = bacc.Bacc("TRN2", target_bir_lowering=False, num_devices=1)
    args = [nc.dram_tensor(n, v.shape, mybir.dt.from_np(v.dtype), kind="ExternalInput").ap() for n, v in arrays.items()]
    args.append(nc.dram_tensor("out", (BATCHES * SEQ, V), F32, kind="ExternalOutput").ap())
    cond_seq_kernel(nc, *args)
    r = run_bass_kernel_spmd(nc, [arrays], core_ids=[0])
    return r.results[0]["out"].reshape(BATCHES, SEQ, V)
```

```python
from contextlib import ExitStack

import concourse.bass as bass
from concourse import mybir


F32 = mybir.dt.float32
F32R = mybir.dt.float32r
I32 = mybir.dt.int32
ALU = mybir.AluOpType
ACT = mybir.ActivationFunctionType
AX_X = mybir.AxisListType.X

P = 128
V = 512
KC = V // P
HID = 4 * V
BN = 256
ROLES = 3
BATCHES, SEQ = 32, 64
HALVES = 2
LAYERS = 2
T = BATCHES * SEQ // HALVES
NB = BATCHES // HALVES
TB = 512
NTB = T // TB
TILES = T // P
TPB = TB // P
GH = 256
MC = GH // P
NG = HID // GH
STEPS = NG * NTB
UP_C, UP_M = KC * GH, 2 * KC * GH
DN = MC * V
LOT = UP_M + DN
JOBS = 2 * NG + 4
RP = BN + 3 * V
SCALE = float(V) ** -0.5
EPS = 1e-5
CB1, MB1 = 0, HID // P
BP, CB2, MB2 = 2 * (HID // P), 2 * (HID // P) + KC, 2 * (HID // P) + 2 * KC
NBIAS = 2 * (HID // P) + 3 * KC

HI, LO = 0, 1
PRODUCTS = ((HI, HI), (HI, LO), (LO, HI))


def cond_seq_kernel(nc, x_in, fuse_in, c_in, m_in, down_in, up_in, roles_in, bias_in, codes_in, role_in, out):
    with ExitStack() as ctx:
        def sb(name, shape, dt):
            return ctx.enter_context(nc.sbuf_tensor(name, shape, dt))

        def sem(name):
            return ctx.enter_context(nc.semaphore(name))

        fused = nc.dram_tensor("fused", (2 * LAYERS, P, KC * V), F32, kind="Internal").ap()
        x = sb("x", [P, KC, T], F32)
        acc = sb("acc", [P, KC * T], F32)
        accv = acc[:, :].rearrange("p (k t) -> p k t", k=KC)
        aT = sb("aT", [P, 2, KC, T], F32R)
        aTf = aT[:, :, :, :].rearrange("p s k t -> p s (k t)")
        cT = sb("cT", [P, 2, KC * T], F32R)
        cTv = cT[:, :, :].rearrange("p s (k t) -> p s k t", k=KC)
        slot = [sb(f"slot{i}", [P, 2, LOT], F32R) for i in range(2)]
        raw = sb("raw", [P, LOT], F32)
        hraw = sb("hraw", [P, 2, 512], F32)
        hs = sb("hs", [P, 2, 2, 2, 512], F32R)
        hz = sb("hz", [P, 2, 2, 2, 3, SEQ], F32R)
        rolep = sb("rolep", [P, 2, RP], F32)
        ident = sb("ident", [P, P], F32)
        bias = sb("bias", [P, LAYERS, NBIAS], F32)
        codes_i = sb("codes_i", [P, BATCHES], I32)
        codes = sb("codes", [P, BATCHES], F32)
        feat = sb("feat", [P, KC], F32)
        oh = sb("oh", [P, LAYERS, KC, BATCHES], F32)
        roles = sb("roles", [1, BATCHES], I32)
        mx = sb("mx", [P, TPB], F32)
        rsum = sb("rsum", [P, TPB], F32)
        rinv = sb("rinv", [P, TPB], F32)
        stats = sb("stats", [P, 2, 6], F32)
        mv = sb("mv", [P, 2, 2], F32)
        veps = sb("veps", [P, 2, 1], F32)
        rstd = sb("rstd", [P, 2, 1], F32)
        mhalf = sb("mhalf", [P, 1], F32)
        ps = [ctx.enter_context(nc.psum_tensor(f"ps{i}", [P, 512], F32)) for i in range(8)]

        hflat = hraw[:, :, :].rearrange("p a b -> p (a b)")
        pblk = hflat[:, 0:512].rearrange("p (i k) -> p i k", i=TPB)
        sm = hflat[:, 512:768].rearrange("p (i k) -> p i k", i=TPB)
        ex = hflat[:, 768:1024].rearrange("p (i k) -> p i k", i=TPB)

        def tmp(s, a, n):
            return acc[:, s * 2048 + a:s * 2048 + a + n]

        xc = [tmp(s, 0, 512).rearrange("p (k t) -> p k t", k=KC) for s in range(2)]
        hp = [tmp(s, 1024, 256) for s in range(2)]
        hg = [tmp(s, 1280, 256) for s in range(2)]
        y = [tmp(s, 1536, 512) for s in range(2)]
        xz = [hs[:, s, :, :, :].rearrange("p l m (k b t) -> p l (m k) b t", k=2, b=4) for s in range(2)]

        t_bank = [[ps[i] for i in (2, 3, 4, 5)], [ps[i] for i in (6, 7, 0, 1)]]
        v_bank = [[ps[0], ps[1]], [ps[2], ps[3]]]
        s_bank, pt_bank = [ps[6], ps[4]], [ps[7], ps[5]]
        a_bank = [[ps[i] for i in (2, 3, 4, 5)], [ps[i] for i in (6, 7, 4, 5)]]
        d_bank, u_bank, h_bank = [ps[6], ps[7]], [ps[0], ps[1], ps[5]], ps[2]
        back_bank = [ps[3], ps[4]] * (TILES // 2 - 1) + [ps[6], ps[7]]

        consts_in = sem("consts_in")
        x_loaded = [sem(f"x_loaded{b}") for b in range(NTB)]
        chunk_loaded = [sem(f"chunk_loaded{k}") for k in range(KC)]
        fuse_loaded = [[sem(f"fuse_loaded{n}_{o}") for o in range(2)] for n in range(2 * LAYERS)]
        fuse_hi, fuse_lo, fuse_mm = sem("fuse_hi"), sem("fuse_lo"), sem("fuse_mm")
        fuse_copied, fused_hi, fused_lo = sem("fuse_copied"), sem("fused_hi"), sem("fused_lo")
        fuse_stored = [sem(f"fuse_stored{s}") for s in range(KC)]
        made = sem("made")
        codes_ready, oh_ready = sem("codes_ready"), sem("oh_ready")
        raw_loaded, w_hi, w_lo = sem("raw_loaded"), sem("w_hi"), sem("w_lo")
        xs_hi, xs_lo = sem("xs_hi"), sem("xs_lo")
        t_done, t_hi, t_lo = sem("t_done"), sem("t_hi"), sem("t_lo")
        v_done, v_hi, v_lo = sem("v_done"), sem("v_hi"), sem("v_lo")
        s_done, mx_done, sm_ready, ex_done = sem("s_done"), sem("mx_done"), sem("sm_ready"), sem("ex_done")
        rs_done, ri_done, p_zeroed, p_ready = sem("rs_done"), sem("ri_done"), sem("p_zeroed"), sem("p_ready")
        pt_done, pt_hi, pt_lo = sem("pt_done"), sem("pt_hi"), sem("pt_lo")
        pv_done, a_hi, a_lo = sem("pv_done"), sem("a_hi"), sem("a_lo")
        acc_init = sem("acc_init")
        up_done, h_hi, h_lo, dn_done, acc_done = (sem(n) for n in ("up_done", "h_hi", "h_lo", "dn_done", "acc_done"))
        c_hi, c_lo = sem("c_hi"), sem("c_lo")
        xz_zeroed, xc_done, xz_hi, xz_lo = sem("xz_zeroed"), sem("xc_done"), sem("xz_hi"), sem("xz_lo")
        t1_done, d_done, hp_done, hg_done = (sem(n) for n in ("t1_done", "d_done", "hp_done", "hg_done"))
        t2_done, hz_hi, hz_lo, u_done, y_done = (sem(n) for n in ("t2_done", "hz_hi", "hz_lo", "u_done", "y_done"))
        st_done, ag_done, ve_done, rstd_done = (sem(n) for n in ("st_done", "ag_done", "ve_done", "rstd_done"))
        yn_done, g_done, b_done = sem("yn_done"), sem("g_done"), sem("b_done")
        bd_loaded = [sem(f"bd_loaded{s}") for s in range(2)]
        gb_loaded = [sem(f"gb_loaded{s}") for s in range(2)]
        t3_done, x_back = sem("t3_done"), sem("x_back")
        stored = [sem(f"stored{s}") for s in range(2)]

        def job_qk(p): return JOBS * p
        def job_vp(p): return JOBS * p + 1
        def job_c(p, g): return JOBS * p + 2 + g
        def job_m(p, g): return JOBS * p + 2 + NG + g
        def job_d(p): return JOBS * p + 2 + 2 * NG
        def job_u(p): return JOBS * p + 3 + 2 * NG

        rflat = rolep[:, :, :].rearrange("p a b -> p (a b)")
        fuse_raw = [(acc[:, 0:2048], acc[:, 2048:4096]), (rflat[:, 0:2048], raw[:, 0:2048])]
        fuse_parts = [(aTf[:, :, 0:2048], aTf[:, :, 2048:4096]), (slot[0][:, :, 0:2048], slot[1][:, :, 0:2048])]
        fuse_bank = [ps[0:4], ps[4:8]]
        stage = [buf[:, a:a + V] for buf in (rflat, raw) for a in (2048, 2048 + V)]

        def fuse_n(n):
            return 2 * (KC + n)

        fused_steps = (1, 2, 4, 5)

        def hp_n(e): return e + 3
        def b_n(e): return e + 3

        def fused_w(w, part):
            return cT[:, part, w * 2048:(w + 1) * 2048].rearrange("p (k n) -> p k n", k=KC)

        block = ctx.enter_context(nc.Block())

        @block.sync
        def _(sp):
            for k in range(KC):
                for o in range(2):
                    sp.dma_start(fuse_raw[0][o][:, k * V:(k + 1) * V], fuse_in[0, o, :, k * V:(k + 1) * V]).then_inc(chunk_loaded[k], 16)
            for n in range(1, 2 * LAYERS):
                if n >= 2:
                    sp.wait_ge(fuse_lo, fuse_n(n - 2))
                for o in range(2):
                    sp.dma_start(fuse_raw[n % 2][o], fuse_in[n, o]).then_inc(fuse_loaded[n][o], 16)
                if n == 1:
                    sp.dma_start(bias[:, :, :], bias_in).then_inc(consts_in, 16)
                    sp.dma_start(codes_i[:, :], codes_in).then_inc(consts_in, 16)
                    sp.dma_start(roles[:, :], role_in).then_inc(consts_in, 16)
            for b in range(NTB):
                sp.dma_start(x[:, :, b * TB:(b + 1) * TB], x_in[0, b]).then_inc(x_loaded[b], 16)
            for q in range(KC * 2 * LAYERS):
                sp.wait_ge(fuse_copied, q + 1)
                sp.dma_start(fused[q // KC, :, (q % KC) * V:(q % KC + 1) * V], stage[q % KC]).then_inc(fuse_stored[q % KC], 16)
            for s in range(KC):
                sp.wait_ge(fuse_stored[s], 16 * 2 * LAYERS)
            sp.wait_ge(consts_in, 48)

            def load_job(job, src, n):
                if isinstance(job, int) and job == 2:
                    return
                sp.wait_ge(w_lo, job)
                sp.dma_start(raw[:, 0:n], src).then_inc(raw_loaded, 16)

            def load_role(layer, half, i, cols, loaded):
                sp.nop(nofuse=True)
                for b in range(2):
                    r = sp.value_load(roles[0:1, bass.ds(half * NB + 2 * i + b, 1)], min_val=0, max_val=ROLES - 1)
                    sp.dma_start(rolep[b * SEQ:(b + 1) * SEQ, i % 2, cols],
                                 roles_in[layer, bass.ds(r, 1), cols].to_broadcast([SEQ, cols.stop - cols.start])).then_inc(loaded[i % 2], 16)

            with sp.Fori(0, HALVES) as half:
                for layer in range(LAYERS):
                    p = 2 * half + layer

                    def load_bd(i):
                        sp.wait_ge(hp_done, hp_n(8 * p + i - 2))
                        load_role(layer, half, i, slice(0, BN), bd_loaded)

                    def load_gb(i):
                        sp.wait_ge(b_done, b_n(8 * p + i - 2))
                        load_role(layer, half, i, slice(BN, RP), gb_loaded)

                    def store(i):
                        if layer == 1:
                            sp.wait_ge(b_done, b_n(8 * p + i))
                            sp.dma_start(out[bass.ds(half * T + i * P, P), :], y[i % 2]).then_inc(stored[i % 2], 16)

                    def next_x(b):
                        if layer == 1:
                            sp.wait_ge(xc_done, 8 * p + TPB * (b + 1))
                            sp.nop(nofuse=True)
                            with sp.If(half < HALVES - 1):
                                sp.dma_start(x[:, :, b * TB:(b + 1) * TB], x_in[1, b]).then_inc(x_loaded[b], 16)

                    load_job(job_c(p, 0), c_in[layer, 0], UP_C + DN)
                    for i in range(2):
                        load_bd(i)
                        load_gb(i)
                    with sp.Fori(1, NG) as g:
                        load_job(job_c(p, g), c_in[layer, bass.ds(g, 1)].rearrange("o p n -> p (o n)"), UP_C + DN)
                    with sp.Fori(0, NG) as g:
                        load_job(job_m(p, g), m_in[layer, bass.ds(g, 1)].rearrange("o p n -> p (o n)"), LOT)
                    load_job(job_d(p), down_in[layer], LOT)
                    load_job(job_u(p), up_in[layer], LOT)
                    nxt = 2 * layer
                    load_bd(2)
                    load_bd(3)
                    load_job(job_qk(p + 1), fused[nxt], 2048)
                    load_bd(4)
                    for i in range(TILES):
                        store(i)
                        if i < TILES - 2:
                            load_gb(i + 2)
                        if i < TILES - 5:
                            load_bd(i + 5)
                        if i == 0:
                            load_job(job_vp(p + 1), fused[nxt + 1], 2048)
                        if i in (1, 4):
                            next_x(i // 4)
            for s in range(2):
                sp.wait_ge(stored[s], 16 * HALVES * TILES // 2)

        @block.gpsimd
        def _(pool):
            nc.gpsimd.memset(ident[:, :], 0.0).then_inc(made, 1)
            nc.gpsimd.iota(feat[:, :], [[P, KC]], base=0, channel_multiplier=1,
                           allow_small_or_imprecise_dtypes=True).then_inc(made, 1)
            nc.gpsimd.memset(mhalf[:, :], -0.5).then_inc(made, 1)
            pool.wait_ge(made, 1)
            nc.gpsimd.affine_select(out=ident[:, :], in_=ident[:, :], compare_op=ALU.not_equal, fill=1.0,
                                    base=0, pattern=[[-1, P]], channel_multiplier=1).then_inc(made, 1)
            for s in range(2):
                for a, free in ((HI, hp_done), (LO, b_done)):
                    nc.gpsimd.memset(hz[:, s, a, :, 1, :].bitcast(F32), 0.0).then_inc(free, 1)


            with pool.Fori(0, HALVES) as half:
                for layer in range(LAYERS):
                    p = 2 * half + layer
                    pool.wait_ge(xs_lo, 2 * KC * p + 1)
                    pool.wait_ge(oh_ready, LAYERS * KC)
                    pool.nop(nofuse=True)
                    nc.gpsimd.memset(pblk, 0.0).then_inc(p_zeroed, 1)
                    if layer == 1:
                        pool.wait_ge(t3_done, 8 * (half + 1))
                    for k in range(KC):
                        nc.gpsimd.tensor_copy(accv[:, k, :].rearrange("p (b t) -> p b t", b=NB),
                                              oh[:, layer, k, bass.ds(half * NB, NB)].unsqueeze(2).to_broadcast([P, NB, SEQ])
                                              ).then_inc(acc_init, 1)
                    for s in range(2):
                        pool.wait_ge(dn_done, 128 * p + 124 + 4 * s)
                        pool.nop(nofuse=True)
                        nc.gpsimd.memset(hs[:, s, :, :, :].rearrange("p l m (k b t) -> p (l m k) b t", k=2, b=4)[:, :, 1, :].bitcast(F32), 0.0).then_inc(xz_zeroed, 1)
                    with pool.Fori(0, TILES // 2) as pair:
                        for s in range(2):
                            e = 8 * p + 2 * pair + s
                            pool.wait_ge(ve_done, e + 1)
                            nc.gpsimd.tensor_tensor(rstd[:, s, :], veps[:, s, :], mhalf[:, :], ALU.pow).then_inc(rstd_done, 1)
                            pool.wait_ge(gb_loaded[s], 32 * (4 * p + pair + 1))
                            pool.wait_ge(yn_done, e + 1)
                            nc.gpsimd.tensor_tensor(y[s], y[s], rolep[:, s, BN + V:BN + 2 * V], ALU.mult).then_inc(g_done, 1)
                            pool.wait_ge(g_done, e + 1)
                            nc.gpsimd.tensor_tensor(y[s], y[s], rolep[:, s, BN + 2 * V:BN + 3 * V], ALU.add).then_inc(b_done, 1)
                    if layer == 1:
                        for s in range(2):
                            pool.wait_ge(stored[s], 16 * (TILES // 2) * (half + 1))

        @block.tensor
        def _(pe):
            pe.wait_ge(made, 4)

            def product(out, pairs, start=True, stop=True):
                n, total = 0, 3 * len(pairs)
                for lhs, rhs, wait in pairs:
                    if wait is not None:
                        pe.wait_ge(*wait)
                    for a, b in PRODUCTS:
                        mm = nc.tensor.matmul(out, lhs(a), rhs(b), start=(start and n == 0), stop=(stop and n == total - 1))
                        n += 1
                return mm

            for k in range(KC):
                pe.wait_ge(fuse_lo, 2 * (k + 1))
                u, w = fuse_parts[0]
                for c in range(KC):
                    mm = product(fuse_bank[0][c][:, :], [(lambda a: u[:, a, k * V + c * P:k * V + (c + 1) * P],
                                                          lambda a: w[:, a, k * V:(k + 1) * V], None)], k == 0, k == KC - 1)
                    if k == KC - 1:
                        mm.then_inc(fuse_mm, 1)
            for n in range(1, 2 * LAYERS):
                pe.wait_ge(fuse_lo, fuse_n(n))
                u, w = fuse_parts[n % 2]
                for c in range(KC):
                    if n >= 2:
                        pe.wait_ge(fuse_copied, KC * (n - 2) + c + 1)
                    product(fuse_bank[n % 2][c][:, :], [
                        (lambda a, k=k: u[:, a, k * V + c * P:k * V + (c + 1) * P], lambda a, k=k: w[:, a, k * V:(k + 1) * V], None)
                        for k in range(KC)]).then_inc(fuse_mm, 1)
            pe.wait_ge(consts_in, 48)

            def attention(p, half, layer, b):
                cols = slice(b * TB, (b + 1) * TB)
                if b == 0:
                    pe.wait_ge(w_lo, job_qk(p) + 1)
                for j in range(KC):
                    if b == 0 and j == 2:
                        pe.wait_ge(w_lo, job_vp(p) + 1)
                    if b == 0 and layer == 1 and j in (1, 2):
                        pe.wait_ge(x_back, 8 * half + 4 + j)
                    product(t_bank[b][j][:, :], [
                        (lambda a, k=k: fused_w(0, a)[:, k, j * P:(j + 1) * P], lambda c, k=k: aT[:, c, k, cols],
                         (xs_lo, 8 * p + KC * b + k + 1) if j == 0 else None) for k in range(KC)]).then_inc(t_done, 1)
                    if b == 0 and layer == 1 and j % 2:
                        turn_back(p - 1, half, TILES - 2 + j // 2)
                if b == 0:
                    pe.wait_ge(t_lo, 8 * p + 1)

                def values(i):
                    if b == 1 and i < 2:
                        pe.wait_ge(a_lo, 8 * p + i + 1)
                    if i >= 2:
                        pe.wait_ge(v_lo, 8 * p + TPB * b + i - 1)
                    product(v_bank[b][i % 2][:, :], [
                        (lambda a, k=k: aT[:, a, k, b * TB + i * P:b * TB + (i + 1) * P], lambda c, k=k: fused_w(1, c)[:, k, :], None)
                        for k in range(KC)]).then_inc(v_done, 1)

                def scores():
                    if b == 1:
                        pe.wait_ge(a_lo, 8 * p + 3)
                    elif layer == 1:
                        pe.wait_ge(x_back, 8 * half + TILES - 1)
                    for i in range(TPB):
                        mm = product(s_bank[b][:, i * P:(i + 1) * P], [
                            (lambda a, j=j: hs[:, j // 2, a, j % 2, i * P:(i + 1) * P],
                             lambda c, j=j: aT[:, c, j, b * TB + i * P:b * TB + (i + 1) * P],
                             (t_lo, 8 * p + KC * b + j + 1) if i == 0 else None) for j in range(KC)])
                    mm.then_inc(s_done, 1)

                values(0)
                scores()
                values(1)
                values(2)
                pe.wait_ge(p_ready, 4 * p + 2 * b + 2)
                if b == 1:
                    pe.wait_ge(a_lo, 8 * p + KC)
                elif layer == 1:
                    pe.wait_ge(x_back, 8 * (half + 1))
                for i in range(TPB):
                    mm = nc.tensor.transpose(pt_bank[b][:, i * P:(i + 1) * P], pblk[:, i, :], ident[:, :])
                mm.then_inc(pt_done, 1)
                values(3)
                pe.wait_ge(pt_lo, 2 * p + b + 1)
                for i in range(TPB):
                    pe.wait_ge(v_lo, 8 * p + TPB * b + i + 1)
                    for f in range(KC):
                        mm = product(a_bank[b][f][:, i * P:(i + 1) * P], [
                            (lambda a: slot[1][:, a, i * V + f * P:i * V + (f + 1) * P],
                             lambda c: slot[1][:, c, 2048 + i * P:2048 + (i + 1) * P], None)])
                        if i == TPB - 1:
                            mm.then_inc(pv_done, 1)

            def up(p, r, kind, g_job, s, b):
                kin = KC * (1 + kind)
                if b == 0:
                    pe.wait_ge(w_lo, g_job + 1)
                for m in range(MC):
                    if not (kind == 0 and isinstance(r, int) and r == 0):
                        pe.wait_ge(h_hi, 64 * p + 2 * (r - 1) + m + 1)
                    pairs = []
                    for k in range(kin):
                        src = aT if k < KC else cTv
                        wait = None
                        if m == 0 and kind == 0 and k == 0:
                            wait = (a_lo, 8 * p + KC * (b + 1))
                        if m == 0 and kind == 1 and k >= KC:
                            wait = (c_lo, 8 * p + KC * b + k - KC + 1)
                        pairs.append((lambda a, k=k: slot[s][:, a, k * GH + m * P:k * GH + (m + 1) * P],
                                      lambda c, k=k, src=src: src[:, c, k % KC, b * TB:(b + 1) * TB], wait))
                    product(ps[m][:, :], pairs).then_inc(up_done, 1)

            def down(p, r, kind, s, b):
                base = UP_M if kind else UP_C
                for o in range(KC):
                    if not (kind == 0 and isinstance(r, int) and r == 0):
                        pe.wait_ge(acc_done, 128 * p + 4 * (r - 1) + o + 1)
                    product(ps[2 + o][:, :], [
                        (lambda a, m=m: slot[s][:, a, base + m * V + o * P:base + m * V + (o + 1) * P],
                         lambda c, m=m: hs[:, b, c, m, :],
                         (h_lo, 64 * p + 2 * r + m + 1) if o == 0 else None) for m in range(MC)]).then_inc(dn_done, 1)

            def mlp(p, kind):
                job = job_m if kind else job_c
                first = STEPS * kind
                up(p, first, kind, job(p, 0), 0, 0)

                def four(g0, last):
                    for t in range(4):
                        r = first + 2 * g0 + t
                        if not (last and t == 3):
                            n = t + 1
                            up(p, r + 1, kind, job(p, g0 + n // 2), (n // 2) % 2, n % 2)
                        down(p, r, kind, (t // 2) % 2, t % 2)

                if kind == 0:
                    four(0, False)
                    with pe.Fori(1, NG // 2 - 1) as gp:
                        four(2 * gp, False)
                else:
                    with pe.Fori(0, NG // 2 - 1) as gp:
                        four(2 * gp, False)
                four(NG - 2, True)

            def tile_roles(half, i):
                pe.nop(nofuse=True)
                return [pe.value_load(roles[0:1, bass.ds(half * NB + 2 * i + b, 1)], min_val=0, max_val=ROLES - 1)
                        for b in range(2)]

            def front(p, half, i):
                e, s = 8 * p + i, i % 2
                r = tile_roles(half, i)
                if i == 0:
                    pe.wait_ge(w_lo, job_d(p) + 1)
                if i < 2:
                    pe.wait_ge(xz_zeroed, 2 * p + i + 1)
                else:
                    pe.wait_ge(hp_done, hp_n(e - 2))
                pe.wait_ge(xz_lo, e + 1)
                n = 0
                for b in range(2):
                    for k in range(KC):
                        for a, c in PRODUCTS:
                            mm = nc.tensor.matmul(d_bank[s][:, 0:BN], xz[s][:, a, k, b:b + 2, :],
                                                  slot[0][:, c, bass.ds(r[b] * (KC * BN) + k * BN, BN)],
                                                  start=(n == 0), stop=(n == 6 * KC - 1))
                            n += 1
                mm.then_inc(d_done, 1)
                if i >= 3:
                    pe.wait_ge(y_done, e - 2)
                for k in range(KC):
                    mm = nc.tensor.matmul(u_bank[i % 3][:, k * P:(k + 1) * P], xc[s][:, k, :], ident[:, :], start=(k == 0), stop=False)
                mm.then_inc(t1_done, 1)

            def turn_h(p, i):
                e, s = 8 * p + i, i % 2
                pe.wait_ge(hg_done, e + 1)
                if i == 0:
                    pe.wait_ge(acc_done, 128 * p + 128)
                else:
                    pe.wait_ge(hz_lo, e)
                for k in range(2):
                    mm = nc.tensor.transpose(h_bank[:, k * P:(k + 1) * P], hg[s][:, k * P:(k + 1) * P], ident[:, :])
                mm.then_inc(t2_done, 1)

            def adapter_up(p, half, i):
                e, s = 8 * p + i, i % 2
                r = tile_roles(half, i)
                if i == 0:
                    pe.wait_ge(w_lo, job_u(p) + 1)
                pe.wait_ge(hz_lo, e + 1)
                n = 0
                for b in range(2):
                    for k in range(2):
                        for a, c in PRODUCTS:
                            mm = nc.tensor.matmul(u_bank[i % 3][:, :], hz[:, s, a, k, b:b + 2, :],
                                                  slot[1][:, c, bass.ds(r[b] * (2 * V) + k * V, V)],
                                                  start=False, stop=(n == 11))
                            n += 1
                mm.then_inc(u_done, 1)

            def turn_back(p, half, i):
                pe.wait_ge(b_done, b_n(8 * p + i))
                if 2 <= i < TILES - 2:
                    pe.wait_ge(x_back, 8 * half + i - 1)
                for k in range(KC):
                    mm = nc.tensor.transpose(back_bank[i][:, k * P:(k + 1) * P], y[i % 2][:, k * P:(k + 1) * P], ident[:, :])
                mm.then_inc(t3_done, 1)

            with pe.Fori(0, HALVES) as half:
                for layer in range(LAYERS):
                    p = 2 * half + layer
                    for b in range(NTB):
                        attention(p, half, layer, b)
                    mlp(p, 0)
                    mlp(p, 1)
                    front(p, half, 0)
                    front(p, half, 1)
                    turn_h(p, 0)
                    for i in range(TILES):
                        if i + 2 < TILES:
                            front(p, half, i + 2)
                        if i + 1 < TILES:
                            turn_h(p, i + 1)
                        if layer == 0 and 2 <= i < TILES - 1:
                            turn_back(p, half, i - 2)
                        adapter_up(p, half, i)
                    if layer == 0:
                        turn_back(p, half, TILES - 3)

        @block.scalar
        def _(act):
            def split_hi(job, n, dst, *free):
                act.wait_ge(raw_loaded, 16 * (job - 1))
                for w in free:
                    act.wait_ge(*w)
                nc.scalar.activation(dst, raw[:, 0:n], ACT.Copy).then_inc(w_hi, 1)

            def operands(n):
                if n == 0:
                    for k in range(KC):
                        act.wait_ge(chunk_loaded[k], 32)
                        for o in range(2):
                            cols = slice(k * V, (k + 1) * V)
                            nc.scalar.activation(fuse_parts[0][o][:, HI, cols], fuse_raw[0][o][:, cols], ACT.Copy).then_inc(fuse_hi, 1)
                    return
                if n >= 2:
                    act.wait_ge(fuse_mm, KC * (n - 1))
                for o in range(2):
                    act.wait_ge(fuse_loaded[n][o], 16)
                    nc.scalar.activation(fuse_parts[n % 2][o][:, HI, :], fuse_raw[n % 2][o], ACT.Copy).then_inc(fuse_hi, 1)

            def results(n):
                for c in range(KC):
                    q = KC * n + c
                    act.wait_ge(fuse_mm, q + 1)
                    if n >= 2:
                        nc.scalar.activation(cT[:, HI, 2048 * (n - 2) + c * V:2048 * (n - 2) + (c + 1) * V],
                                             fuse_bank[n % 2][c][:, :], ACT.Copy)
                    if n >= 1:
                        act.wait_ge(fuse_stored[c], 16 * n)
                    nc.scalar.activation(stage[c], fuse_bank[n % 2][c][:, :], ACT.Copy).then_inc(fuse_copied, 1)

            def split_block(p, half, layer, b, k):
                if layer == 0:
                    act.wait_ge(x_loaded[b], 16 * (half + 1))
                else:
                    act.wait_ge(x_back, 8 * half + TPB * (b + 1))
                cols = slice(b * TB, (b + 1) * TB)
                nc.scalar.activation(aT[:, HI, k, cols], x[:, k, cols], ACT.Copy).then_inc(xs_hi, 1)

            for n in range(3):
                operands(n)
            results(0)
            operands(3)
            results(1)
            results(2)
            for k in range(KC):
                split_block(0, 0, 0, 0, k)
            results(3)
            act.wait_ge(consts_in, 48)

            def back(half, i):
                act.wait_ge(t3_done, 8 * half + i + 1)
                nc.scalar.activation(x[:, :, i * P:(i + 1) * P], back_bank[i][:, :].rearrange("p (k t) -> p k t", k=KC),
                                     ACT.Copy).then_inc(x_back, 1)

            def attention(p, half, layer, b):
                cols = slice(b * TB, (b + 1) * TB)
                for j in range(KC):
                    act.wait_ge(t_done, 8 * p + KC * b + j + 1)
                    nc.scalar.activation(hs[:, j // 2, HI, j % 2, :], t_bank[b][j][:, :], ACT.Copy).then_inc(t_hi, 1)
                    if b == 0 and layer == 1 and j % 2:
                        back(half, TILES - 2 + j // 2)

                def values(i):
                    act.wait_ge(v_done, 8 * p + TPB * b + i + 1)
                    nc.scalar.activation(slot[1][:, HI, i * V:(i + 1) * V], v_bank[b][i % 2][:, :], ACT.Copy).then_inc(v_hi, 1)

                values(0)
                if b == 0:
                    for k in range(KC):
                        split_block(p, half, layer, 1, k)
                act.wait_ge(sm_ready, 4 * p + 2 * b + 2)
                nc.scalar.activation(ex, sm, ACT.Exp, scale=SCALE).then_inc(ex_done, 1)
                values(1)
                values(2)
                act.wait_ge(pt_done, 2 * p + b + 1)
                nc.scalar.activation(slot[1][:, HI, 2048:2560], pt_bank[b][:, :], ACT.Copy).then_inc(pt_hi, 1)
                values(3)
                for f in range(KC):
                    act.wait_ge(pv_done, 8 * p + KC * b + f + 1)
                    nc.scalar.activation(aT[:, HI, f, cols], a_bank[b][f][:, :], ACT.Identity,
                                         bias=bias[:, layer, BP + f:BP + f + 1]).then_inc(a_hi, 1)
                if b == 0:
                    split_hi(job_c(p, 0), UP_C + DN, slot[0][:, HI, 0:UP_C + DN])

            def hidden(p, layer, kind, r, g, b):
                for m in range(MC):
                    act.wait_ge(up_done, 64 * p + 2 * r + m + 1)
                    early = kind == 0 and isinstance(r, int)
                    if not (early and r == 0):
                        act.wait_ge(h_lo, 64 * p + 2 * (r - 1) + m + 1)
                    if not (early and r < 2):
                        act.wait_ge(dn_done, 128 * p + 4 * (r - 1))
                    col = (MB1 if kind else CB1) + MC * g + m
                    b1 = bias[:, layer, bass.ds(col, 1)]
                    act.nop(nofuse=True)
                    nc.scalar.activation(hraw[:, m, :], ps[m][:, :], ACT.Gelu, bias=b1)
                    nc.scalar.activation(hs[:, b, HI, m, :], ps[m][:, :], ACT.Gelu, bias=b1).then_inc(h_hi, 1)

            def mlp(p, layer, kind):
                n = LOT if kind else UP_C + DN
                job = job_m if kind else job_c
                first = STEPS * kind

                def group(g, s, nxt, first_c=False):
                    r = first + 2 * g
                    hidden(p, layer, kind, r, g, 0)
                    if nxt:
                        free = (pv_done, 8 * p + 8) if first_c else (dn_done, 128 * p + 4 * r)
                        split_hi(job(p, g + 1), n, slot[1 - s][:, HI, 0:n], free)
                    elif kind == 0:
                        split_hi(job_m(p, 0), LOT, slot[0][:, HI, 0:LOT], (dn_done, 128 * p + 4 * r))
                    else:
                        split_hi(job_d(p), LOT, slot[0][:, HI, 0:LOT], (dn_done, 128 * p + 4 * r))
                    hidden(p, layer, kind, r + 1, g, 1)

                if kind == 0:
                    group(0, 0, True, True)
                    group(1, 1, True)
                    with act.Fori(1, NG // 2 - 1) as gp:
                        group(2 * gp, 0, True)
                        group(2 * gp + 1, 1, True)
                else:
                    with act.Fori(0, NG // 2 - 1) as gp:
                        group(2 * gp, 0, True)
                        group(2 * gp + 1, 1, True)
                group(NG - 2, 0, True)
                group(NG - 1, 1, False)

            with act.Fori(0, HALVES) as half:
                for layer in range(LAYERS):
                    p = 2 * half + layer
                    for b in range(NTB):
                        attention(p, half, layer, b)
                    mlp(p, layer, 0)
                    for b in range(NTB):
                        for o in range(KC):
                            act.wait_ge(acc_done, 128 * p + 4 * (STEPS - 2 + b) + o + 1)
                            nc.scalar.activation(cTv[:, HI, o, b * TB:(b + 1) * TB], accv[:, o, b * TB:(b + 1) * TB],
                                                 ACT.Copy).then_inc(c_hi, 1)
                    mlp(p, layer, 1)

                    def split_x(i):
                        e, s = 8 * p + i, i % 2
                        act.wait_ge(xc_done, e + 1)
                        if i < 2:
                            act.wait_ge(dn_done, 128 * p + 124 + 4 * i)
                        else:
                            act.wait_ge(d_done, e - 1)
                        nc.scalar.activation(xz[s][:, HI, :, 0:3:2, :], xc[s].rearrange("p k (b t) -> p k b t", b=2),
                                             ACT.Copy).then_inc(xz_hi, 1)

                    def gelu_h(i):
                        act.wait_ge(hp_done, hp_n(8 * p + i))
                        nc.scalar.activation(hg[i % 2], hp[i % 2], ACT.Gelu).then_inc(hg_done, 1)

                    def split_h(i):
                        act.wait_ge(t2_done, 8 * p + i + 1)
                        nc.scalar.activation(hz[:, i % 2, HI, :, 0:3:2, :], h_bank[:, 0:BN].rearrange("p (k b t) -> p k b t", k=2, b=2),
                                             ACT.Copy).then_inc(hz_hi, 1)

                    def fused_hi_part(q):
                        act.wait_ge(raw_loaded, 16 * (job_qk(p + 1) + q // 2 - 1))
                        nc.scalar.activation(cT[:, HI, 1024 * q:1024 * (q + 1)], raw[:, 1024 * (q % 2):1024 * (q % 2 + 1)],
                                             ACT.Copy).then_inc(w_hi if q % 2 else fused_hi, 1)

                    split_x(0)
                    split_x(1)
                    split_hi(job_u(p), LOT, slot[1][:, HI, 0:LOT])
                    gelu_h(0)
                    split_x(2)
                    gelu_h(1)
                    split_h(0)
                    for i in range(TILES):
                        if i + 3 < TILES:
                            split_x(i + 3)
                        if i + 2 < TILES:
                            gelu_h(i + 2)
                        if i + 1 < TILES:
                            split_h(i + 1)
                        if layer == 0 and 2 <= i < TILES - 1:
                            back(half, i - 2)
                        if i in fused_steps:
                            fused_hi_part(fused_steps.index(i))
                        if i == TILES - 2:
                            if layer == 0:
                                for k in range(KC):
                                    split_block(p + 1, half, 1, 0, k)
                            else:
                                act.nop(nofuse=True)
                                with act.If(half < HALVES - 1):
                                    for k in range(KC):
                                        split_block(p + 1, half + 1, 0, 0, k)
                    if layer == 0:
                        back(half, TILES - 3)

        @block.vector
        def _(dve):
            def minus(out, a, hi):
                return nc.vector.tensor_tensor(out, a, hi.bitcast(F32), ALU.subtract)

            def split_lo(job, n, dst):
                dve.wait_ge(w_hi, job - 1)
                minus(dst[:, LO, :], raw[:, 0:n], dst[:, HI, :]).then_inc(w_lo, 1)

            def operands(n):
                if n == 0:
                    for k in range(KC):
                        for o in range(2):
                            dve.wait_ge(fuse_hi, 2 * k + o + 1)
                            u, cols = fuse_parts[0][o], slice(k * V, (k + 1) * V)
                            minus(u[:, LO, cols], fuse_raw[0][o][:, cols], u[:, HI, cols]).then_inc(fuse_lo, 1)
                    return
                for o in range(2):
                    dve.wait_ge(fuse_hi, fuse_n(n) - 1 + o)
                    u = fuse_parts[n % 2][o]
                    minus(u[:, LO, :], fuse_raw[n % 2][o], u[:, HI, :]).then_inc(fuse_lo, 1)

            def results(n):
                for c in range(KC):
                    dve.wait_ge(fuse_copied, KC * n + c + 1)
                    cols = slice(2048 * (n - 2) + c * V, 2048 * (n - 2) + (c + 1) * V)
                    mm = minus(cT[:, LO, cols], fuse_bank[n % 2][c][:, :], cT[:, HI, cols])
                    mm.then_inc(w_lo if c == KC - 1 else fused_lo, 1)

            operands(0)
            operands(1)
            dve.wait_ge(consts_in, 48)
            nc.vector.tensor_copy(codes[:, :], codes_i[:, :]).then_inc(codes_ready, 1)
            dve.wait_ge(codes_ready, 1)
            dve.wait_ge(made, 4)
            for layer in range(LAYERS):
                for k in range(KC):
                    nc.vector.tensor_scalar(oh[:, layer, k, :], codes[:, :], feat[:, k:k + 1],
                                            bias[:, layer, CB2 + k:CB2 + k + 1], ALU.is_equal, ALU.add).then_inc(oh_ready, 1)
            operands(2)
            operands(3)
            results(2)

            def split_block(p, b, k):
                dve.wait_ge(xs_hi, 8 * p + KC * b + k + 1)
                cols = slice(b * TB, (b + 1) * TB)
                minus(aT[:, LO, k, cols], x[:, k, cols], aT[:, HI, k, cols]).then_inc(xs_lo, 1)

            for k in range(KC):
                split_block(0, 0, k)
            results(3)

            def attention(p, layer, b):
                cols = slice(b * TB, (b + 1) * TB)
                for j in range(KC):
                    dve.wait_ge(t_hi, 8 * p + KC * b + j + 1)
                    minus(hs[:, j // 2, LO, j % 2, :], t_bank[b][j][:, :], hs[:, j // 2, HI, j % 2, :]).then_inc(t_lo, 1)
                def values(i):
                    dve.wait_ge(v_hi, 8 * p + TPB * b + i + 1)
                    minus(slot[1][:, LO, i * V:(i + 1) * V], v_bank[b][i % 2][:, :], slot[1][:, HI, i * V:(i + 1) * V]).then_inc(v_lo, 1)

                values(0)
                if b == 0:
                    for k in range(KC):
                        split_block(p, 1, k)
                diag = [s_bank[b][h * SEQ:(h + 1) * SEQ, :].rearrange("p (i h k) -> p i h k", i=TPB, h=2)[:, :, h, :] for h in range(2)]
                rows = [slice(h * SEQ, (h + 1) * SEQ) for h in range(2)]
                dve.wait_ge(s_done, 2 * p + b + 1)
                for h in range(2):
                    nc.vector.tensor_reduce(mx[rows[h], :], diag[h], AX_X, ALU.max).then_inc(mx_done, 1)
                for h in range(2):
                    dve.wait_ge(mx_done, 4 * p + 2 * b + h + 1)
                    nc.vector.tensor_tensor(sm[rows[h], :, :], diag[h], mx[rows[h], :].unsqueeze(2).to_broadcast([SEQ, TPB, SEQ]),
                                            ALU.subtract).then_inc(sm_ready, 1)
                dve.wait_ge(ex_done, 2 * p + b + 1)
                nc.vector.tensor_reduce(rsum[:, :], ex, AX_X, ALU.add).then_inc(rs_done, 1)
                dve.wait_ge(rs_done, 2 * p + b + 1)
                nc.vector.reciprocal(rinv[:, :], rsum[:, :]).then_inc(ri_done, 1)
                dve.wait_ge(ri_done, 2 * p + b + 1)
                dve.wait_ge(p_zeroed, p + 1)
                for h in range(2):
                    nc.vector.tensor_tensor(pblk[rows[h], :, h * SEQ:(h + 1) * SEQ], ex[rows[h], :, :],
                                            rinv[rows[h], :].unsqueeze(2).to_broadcast([SEQ, TPB, SEQ]), ALU.mult).then_inc(p_ready, 1)
                values(1)
                values(2)
                dve.wait_ge(pt_hi, 2 * p + b + 1)
                minus(slot[1][:, LO, 2048:2560], pt_bank[b][:, :], slot[1][:, HI, 2048:2560]).then_inc(pt_lo, 1)
                values(3)
                for f in range(KC):
                    dve.wait_ge(a_hi, 8 * p + KC * b + f + 1)
                    nc.vector.scalar_tensor_tensor(out=aT[:, LO, f, cols], in0=a_bank[b][f][:, :], scalar=bias[:, layer, BP + f:BP + f + 1],
                                                   in1=aT[:, HI, f, cols].bitcast(F32), op0=ALU.add, op1=ALU.subtract).then_inc(a_lo, 1)
                if b == 0:
                    split_lo(job_c(p, 0), UP_C + DN, slot[0][:, :, 0:UP_C + DN])

            def hidden(p, r, b):
                for m in range(MC):
                    dve.wait_ge(h_hi, 64 * p + 2 * r + m + 1)
                    minus(hs[:, b, LO, m, :], hraw[:, m, :], hs[:, b, HI, m, :]).then_inc(h_lo, 1)

            def add(p, kind, r, b):
                for o in range(KC):
                    dve.wait_ge(dn_done, 128 * p + 4 * r + o + 1)
                    dst = (x[:, o, :] if kind else accv[:, o, :])[:, b * TB:(b + 1) * TB]
                    nc.vector.tensor_tensor(dst, ps[2 + o][:, :], dst, ALU.add).then_inc(acc_done, 1)

            def mlp(p, kind):
                n = LOT if kind else UP_C + DN
                job = job_m if kind else job_c
                first = STEPS * kind
                hidden(p, first, 0)

                def group(g, s, nxt):
                    r = first + 2 * g
                    if nxt:
                        split_lo(job(p, g + 1), n, slot[1 - s][:, :, 0:n])
                    elif kind == 0:
                        split_lo(job_m(p, 0), LOT, slot[0][:, :, 0:LOT])
                    else:
                        split_lo(job_d(p), LOT, slot[0][:, :, 0:LOT])
                    hidden(p, r + 1, 1)
                    add(p, kind, r, 0)
                    if nxt:
                        hidden(p, r + 2, 0)
                        add(p, kind, r + 1, 1)

                with dve.Fori(0, NG // 2 - 1) as gp:
                    group(2 * gp, 0, True)
                    group(2 * gp + 1, 1, True)
                group(NG - 2, 0, True)
                group(NG - 1, 1, False)

            with dve.Fori(0, HALVES) as half:
                for layer in range(LAYERS):
                    p = 2 * half + layer
                    for b in range(NTB):
                        attention(p, layer, b)
                    dve.wait_ge(acc_init, KC * (p + 1))
                    mlp(p, 0)
                    for b in range(NTB):
                        cols = slice(b * TB, (b + 1) * TB)
                        if b == 1:
                            add(p, 0, STEPS - 1, 1)
                        for o in range(KC):
                            dve.wait_ge(acc_done, 128 * p + 4 * (STEPS - 2 + b) + o + 1)
                            nc.vector.scalar_tensor_tensor(out=x[:, o, cols], in0=accv[:, o, cols], scalar=bias[:, layer, MB2 + o:MB2 + o + 1],
                                                           in1=x[:, o, cols], op0=ALU.add, op1=ALU.add)
                            dve.wait_ge(c_hi, 8 * p + KC * b + o + 1)
                            minus(cTv[:, LO, o, cols], accv[:, o, cols], cTv[:, HI, o, cols]).then_inc(c_lo, 1)
                    mlp(p, 1)

                    def clip(i):
                        if i >= 2:
                            dve.wait_ge(t1_done, 8 * p + i - 1)
                        nc.vector.tensor_scalar(xc[i % 2], x[:, :, i * P:(i + 1) * P], 0.0, 1.0, ALU.max, ALU.min).then_inc(xc_done, 1)

                    def split_x(i):
                        s = i % 2
                        dve.wait_ge(xz_hi, 8 * p + i + 1)
                        minus(xz[s][:, LO, :, 0:3:2, :], xc[s].rearrange("p k (b t) -> p k b t", b=2), xz[s][:, HI, :, 0:3:2, :]).then_inc(xz_lo, 1)

                    def params(i):
                        return 32 * (4 * p + i // 2 + 1)

                    def h_bias(i):
                        dve.wait_ge(bd_loaded[i % 2], params(i))
                        dve.wait_ge(d_done, 8 * p + i + 1)
                        if i >= 2:
                            dve.wait_ge(hg_done, 8 * p + i - 1)
                        nc.vector.tensor_tensor(hp[i % 2], d_bank[i % 2][:, 0:BN], rolep[:, i % 2, 0:BN], ALU.add).then_inc(hp_done, 1)

                    def split_h(i):
                        s = i % 2
                        dve.wait_ge(hz_hi, 8 * p + i + 1)
                        minus(hz[:, s, LO, :, 0:3:2, :], h_bank[:, 0:BN].rearrange("p (k b t) -> p k b t", k=2, b=2),
                              hz[:, s, HI, :, 0:3:2, :]).then_inc(hz_lo, 1)

                    def row_stats(i):
                        e, s = 8 * p + i, i % 2
                        dve.wait_ge(gb_loaded[s], params(i))
                        dve.wait_ge(u_done, e + 1)
                        if i >= 2:
                            if layer == 0:
                                dve.wait_ge(t3_done, 8 * half + i - 1)
                            else:
                                dve.wait_ge(stored[s], 16 * (4 * half + i // 2))
                        nc.vector.tensor_tensor(y[s], u_bank[i % 3][:, :], rolep[:, s, BN:BN + V], ALU.add).then_inc(y_done, 1)
                        dve.wait_ge(y_done, e + 1)
                        nc.vector.bn_stats(stats[:, s, :], y[s]).then_inc(st_done, 1)
                        dve.wait_ge(st_done, e + 1)
                        dve.nop(nofuse=True)
                        nc.vector.bn_aggr(mv[:, s, :], stats[:, s, :]).then_inc(ag_done, 1)
                        dve.wait_ge(ag_done, e + 1)
                        nc.vector.tensor_scalar(veps[:, s, :], mv[:, s, 1:2], EPS, None, ALU.add).then_inc(ve_done, 1)

                    def normalise(i):
                        s = i % 2
                        dve.wait_ge(rstd_done, 8 * p + i + 1)
                        nc.vector.tensor_scalar(y[s], y[s], mv[:, s, 0:1], rstd[:, s, :], ALU.subtract, ALU.mult).then_inc(yn_done, 1)

                    def fused_lo_part(q):
                        if q % 2:
                            dve.wait_ge(w_hi, job_qk(p + 1) + q // 2 - 1)
                        else:
                            dve.wait_ge(fused_hi, 2 * p + q // 2 + 1)
                        minus(cT[:, LO, 1024 * q:1024 * (q + 1)], raw[:, 1024 * (q % 2):1024 * (q % 2 + 1)],
                              cT[:, HI, 1024 * q:1024 * (q + 1)]).then_inc(w_lo if q % 2 else fused_lo, 1)

                    dve.wait_ge(acc_done, 128 * p + 124)
                    clip(0)
                    split_x(0)
                    clip(1)
                    add(p, 1, 2 * STEPS - 1, 1)
                    split_x(1)
                    h_bias(0)
                    clip(2)
                    split_x(2)
                    dve.wait_ge(w_hi, job_u(p) - 1)
                    minus(slot[1][:, LO, 0:LOT // 2], raw[:, 0:LOT // 2], slot[1][:, HI, 0:LOT // 2])
                    h_bias(1)
                    split_h(0)
                    minus(slot[1][:, LO, LOT // 2:LOT], raw[:, LOT // 2:LOT], slot[1][:, HI, LOT // 2:LOT]).then_inc(w_lo, 1)
                    for i in range(TILES):
                        if i >= 1:
                            row_stats(i - 1)
                        if i + 3 < TILES:
                            if i + 3 == TPB:
                                dve.wait_ge(acc_done, 128 * p + 128)
                            clip(i + 3)
                            split_x(i + 3)
                        if i >= 1:
                            normalise(i - 1)
                        if i + 2 < TILES:
                            h_bias(i + 2)
                        if i + 1 < TILES:
                            split_h(i + 1)
                        if i in fused_steps:
                            fused_lo_part(fused_steps.index(i))
                        if i == TILES - 2:
                            if layer == 0:
                                for k in range(KC):
                                    split_block(p + 1, 0, k)
                            else:
                                dve.nop(nofuse=True)
                                with dve.If(half < HALVES - 1):
                                    for k in range(KC):
                                        split_block(p + 1, 0, k)
                    row_stats(TILES - 1)
                    normalise(TILES - 1)


def _chunks(w):
    import numpy as np
    r, n = w.shape
    return np.ascontiguousarray(w.reshape(r // P, P, n).transpose(1, 0, 2).reshape(P, -1))


def kernel(**inputs):
    import numpy as np
    import concourse.bacc as bacc
    from concourse.bass_utils import run_bass_kernel_spmd

    a = {k: np.asarray(v) for k, v in inputs.items()}
    blocks, adapters = ("L0_cond_", "L2_cond_"), ("L1_cond_", "L3_cond_")
    gains = (("gamma", "beta"), ("ln_w", "ln_b"))

    def groups(w1, w2):
        return np.stack([np.concatenate([_chunks(w1[:, g * GH:(g + 1) * GH]), _chunks(w2[g * GH:(g + 1) * GH])], 1)
                         for g in range(NG)])

    def columns(b):
        return b.reshape(-1, P).T

    arrays = {
        "x_in": np.ascontiguousarray(a["x"].reshape(HALVES, NTB, TB, KC, P).transpose(0, 1, 4, 3, 2)),
        "fuse_in": np.stack([np.stack([_chunks(u), _chunks(w)]) for l in blocks[::-1]
                             for u, w in ((a[l + "Wq"].T, a[l + "Wk"].T), (a[l + "Wv"].T, a[l + "Wp"]))]),
        "c_in": np.stack([groups(a[l + "cW1"], a[l + "cW2"]) for l in blocks]),
        "m_in": np.stack([groups(a[l + "mW1"], a[l + "mW2"]) for l in blocks]),
        "down_in": np.stack([np.concatenate([_chunks(a[l + "W_down"][r]) for r in range(ROLES)], 1) for l in adapters]),
        "up_in": np.stack([np.concatenate([_chunks(a[l + "W_up"][r]) for r in range(ROLES)], 1) for l in adapters]),
        "roles_in": np.stack([np.concatenate([a[l + "b_down"], a[l + "b_up"], a[l + g], a[l + b]], 1)
                              for l, (g, b) in zip(adapters, gains)]),
        "bias_in": np.ascontiguousarray(np.stack([np.concatenate([columns(a[l + n]) for n in ("cb1", "mb1", "bp", "cb2", "mb2")], 1)
                                                  for l in blocks], 1)),
        "codes_in": np.ascontiguousarray(np.broadcast_to(a["itok_B_17_1546"].reshape(1, BATCHES), (P, BATCHES))),
        "role_in": np.ascontiguousarray(a["itok_B_1_2"].reshape(1, BATCHES)),
    }
    nc = bacc.Bacc("TRN2", target_bir_lowering=False, num_devices=1)
    args = [nc.dram_tensor(n, v.shape, mybir.dt.from_np(v.dtype), kind="ExternalInput").ap() for n, v in arrays.items()]
    args.append(nc.dram_tensor("out", (BATCHES * SEQ, V), F32, kind="ExternalOutput").ap())
    cond_seq_kernel(nc, *args)
    r = run_bass_kernel_spmd(nc, [arrays], core_ids=[0])
    return r.results[0]["out"].reshape(BATCHES, SEQ, V)
```

```python
from contextlib import ExitStack

import concourse.bass as bass
from concourse import mybir


F32 = mybir.dt.float32
F32R = mybir.dt.float32r
I32 = mybir.dt.int32
ALU = mybir.AluOpType
ACT = mybir.ActivationFunctionType
AX_X = mybir.AxisListType.X

P = 128
V = 512
KC = V // P
HID = 4 * V
BN = 256
ROLES = 3
BATCHES, SEQ = 32, 64
HALVES = 2
LAYERS = 2
T = BATCHES * SEQ // HALVES
NB = BATCHES // HALVES
TB = 512
NTB = T // TB
TILES = T // P
TPB = TB // P
GH = 256
MC = GH // P
NG = HID // GH
STEPS = NG * NTB
UP_C, UP_M = KC * GH, 2 * KC * GH
DN = MC * V
LOT = UP_M + DN
JOBS = 2 * NG + 4
RP = BN + 3 * V
SCALE = float(V) ** -0.5
EPS = 1e-5
CB1, MB1 = 0, HID // P
BP, CB2, MB2 = 2 * (HID // P), 2 * (HID // P) + KC, 2 * (HID // P) + 2 * KC
NBIAS = 2 * (HID // P) + 3 * KC

HI, LO = 0, 1
PRODUCTS = ((HI, HI), (HI, LO), (LO, HI))


def cond_seq_kernel(nc, x_in, fuse_in, c_in, m_in, down_in, up_in, roles_in, bias_in, codes_in, role_in, out):
    with ExitStack() as ctx:
        def sb(name, shape, dt):
            return ctx.enter_context(nc.sbuf_tensor(name, shape, dt))

        def sem(name):
            return ctx.enter_context(nc.semaphore(name))

        fused = nc.dram_tensor("fused", (2 * LAYERS, P, KC * V), F32, kind="Internal").ap()
        x = sb("x", [P, KC, T], F32)
        acc = sb("acc", [P, KC * T], F32)
        accv = acc[:, :].rearrange("p (k t) -> p k t", k=KC)
        aT = sb("aT", [P, 2, KC, T], F32R)
        aTf = aT[:, :, :, :].rearrange("p s k t -> p s (k t)")
        cT = sb("cT", [P, 2, KC * T], F32R)
        cTv = cT[:, :, :].rearrange("p s (k t) -> p s k t", k=KC)
        slot = [sb(f"slot{i}", [P, 2, LOT], F32R) for i in range(2)]
        raw = sb("raw", [P, LOT], F32)
        hraw = sb("hraw", [P, 2, 512], F32)
        hs = sb("hs", [P, 2, 2, 2, 512], F32R)
        hz = sb("hz", [P, 2, 2, 2, 3, SEQ], F32R)
        rolep = sb("rolep", [P, 2, RP], F32)
        ident = sb("ident", [P, P], F32)
        bias = sb("bias", [P, LAYERS, NBIAS], F32)
        codes_i = sb("codes_i", [P, BATCHES], I32)
        codes = sb("codes", [P, BATCHES], F32)
        feat = sb("feat", [P, KC], F32)
        oh = sb("oh", [P, LAYERS, KC, BATCHES], F32)
        roles = sb("roles", [1, BATCHES], I32)
        mx = sb("mx", [P, TPB], F32)
        rsum = sb("rsum", [P, TPB], F32)
        rinv = sb("rinv", [P, TPB], F32)
        stats = sb("stats", [P, 2, 6], F32)
        mv = sb("mv", [P, 2, 2], F32)
        veps = sb("veps", [P, 2, 1], F32)
        rstd = sb("rstd", [P, 2, 1], F32)
        mhalf = sb("mhalf", [P, 1], F32)
        psum = ctx.enter_context(nc.psum_tensor("psum", [P, 8, 512], F32))
        ps = [psum[:, i, :] for i in range(8)]

        hflat = hraw[:, :, :].rearrange("p a b -> p (a b)")
        pblk = hflat[:, 0:512].rearrange("p (i k) -> p i k", i=TPB)
        sm = hflat[:, 512:768].rearrange("p (i k) -> p i k", i=TPB)
        ex = hflat[:, 768:1024].rearrange("p (i k) -> p i k", i=TPB)

        def tmp(s, a, n):
            return acc[:, s * 2048 + a:s * 2048 + a + n]

        xc = [tmp(s, 0, 512).rearrange("p (k t) -> p k t", k=KC) for s in range(2)]
        hp = [tmp(s, 1024, 256) for s in range(2)]
        hg = [tmp(s, 1280, 256) for s in range(2)]
        y = [tmp(s, a, 512) for a in (1536, 512) for s in range(2)]
        xz = [hs[:, s, :, :, :].rearrange("p l m (k b t) -> p l (m k) b t", k=2, b=4) for s in range(2)]

        t_bank, v_bank, pt_bank = ps[2:6], ps[0:2], ps[7]
        s_bank = ps[6:8]
        a_bank = [ps[2:6], [ps[i] for i in (0, 1, 6, 7)]]
        scores = psum[:, 6:8, :].rearrange("p n (i c k) -> p (n i) c k", i=2, c=2)
        batch_rows = [slice(h * SEQ, (h + 1) * SEQ) for h in range(2)]

        def diagonal(h, c):
            return scores[batch_rows[h], :, c, h * SEQ:(h + 1) * SEQ]

        def a_halves(pair, f):
            return a_bank[pair][f][:, :].rearrange("p (i c q) -> p i c q", i=2, c=2)


        d_bank, u_bank, h_bank = [ps[6], ps[7]], [ps[0], ps[1], ps[5]], ps[2]
        back_bank = [ps[3], ps[4]] * (TILES // 2 - 1) + [ps[6], ps[7]]

        consts_in = sem("consts_in")
        x_loaded = [sem(f"x_loaded{b}") for b in range(NTB)]
        chunk_loaded = [sem(f"chunk_loaded{k}") for k in range(KC)]
        fuse_loaded = [[sem(f"fuse_loaded{n}_{o}") for o in range(2)] for n in range(2 * LAYERS)]
        fuse_hi, fuse_lo, fuse_mm = sem("fuse_hi"), sem("fuse_lo"), sem("fuse_mm")
        fuse_copied, fused_hi, fused_lo = sem("fuse_copied"), sem("fused_hi"), sem("fused_lo")
        fuse_stored = [sem(f"fuse_stored{s}") for s in range(KC)]
        made = sem("made")
        codes_ready, oh_ready = sem("codes_ready"), sem("oh_ready")
        raw_loaded, w_hi, w_lo = sem("raw_loaded"), sem("w_hi"), sem("w_lo")
        xs_hi, xs_lo = sem("xs_hi"), sem("xs_lo")
        t_done, t_hi, t_lo = sem("t_done"), sem("t_hi"), sem("t_lo")
        v_done, v_hi, v_lo = sem("v_done"), sem("v_hi"), sem("v_lo")
        s_done, s_half, ss_done, mx_done, sm_ready, ex_done = (sem(n) for n in ("s_done", "s_half", "ss_done", "mx_done", "sm_ready", "ex_done"))
        rs_done, ri_done, p_zeroed, p_ready = sem("rs_done"), sem("ri_done"), sem("p_zeroed"), sem("p_ready")
        pt_done, pt_hi, pt_lo = sem("pt_done"), sem("pt_hi"), sem("pt_lo")
        pv_done, a_half, a_sum, a_hi, a_lo = sem("pv_done"), sem("a_half"), sem("a_sum"), sem("a_hi"), sem("a_lo")
        acc_init = sem("acc_init")
        up_done, h_hi, h_lo, dn_done, acc_done = (sem(n) for n in ("up_done", "h_hi", "h_lo", "dn_done", "acc_done"))
        c_hi, c_lo = sem("c_hi"), sem("c_lo")
        xz_zeroed, xc_done, xz_hi, xz_lo = sem("xz_zeroed"), sem("xc_done"), sem("xz_hi"), sem("xz_lo")
        t1_done, d_done, hp_done, hg_done = (sem(n) for n in ("t1_done", "d_done", "hp_done", "hg_done"))
        t2_done, hz_hi, hz_lo, u_done, y_done = (sem(n) for n in ("t2_done", "hz_hi", "hz_lo", "u_done", "y_done"))
        st_done, ag_done, ve_done, rstd_done = (sem(n) for n in ("st_done", "ag_done", "ve_done", "rstd_done"))
        yn_done, g_done, b_done = sem("yn_done"), sem("g_done"), sem("b_done")
        bd_loaded = [sem(f"bd_loaded{s}") for s in range(2)]
        gb_loaded = [sem(f"gb_loaded{s}") for s in range(2)]
        t3_done, x_back = sem("t3_done"), sem("x_back")
        stored = [sem(f"stored{s}") for s in range(4)]

        def job_qk(p): return JOBS * p
        def job_vp(p): return JOBS * p + 1
        def job_c(p, g): return JOBS * p + 2 + g
        def job_m(p, g): return JOBS * p + 2 + NG + g
        def job_d(p): return JOBS * p + 2 + 2 * NG
        def job_u(p): return JOBS * p + 3 + 2 * NG

        rflat = rolep[:, :, :].rearrange("p a b -> p (a b)")
        fuse_raw = [(acc[:, 0:2048], acc[:, 2048:4096]), (rflat[:, 0:2048], raw[:, 0:2048])]
        fuse_parts = [(aTf[:, :, 0:2048], aTf[:, :, 2048:4096]), (slot[0][:, :, 0:2048], slot[1][:, :, 0:2048])]
        fuse_bank = [ps[0:4], ps[4:8]]
        a_out = rflat[:, 0:KC * TB].rearrange("p (f t) -> p f t", f=KC)
        a_pair = [[a_out[:, f, i * 256:(i + 1) * 256].rearrange("p (i q) -> p i q", i=2) for f in range(KC)] for i in range(2)]
        stage = [buf[:, a:a + V] for buf in (rflat, raw) for a in (2048, 2048 + V)]

        def fuse_n(n):
            return 2 * (KC + n)

        fused_hi_steps, fused_lo_steps = {1: 0, 2: 1, 4: 2, 5: 3}, {2: 0, 3: 1, 5: 2, 7: 3}

        def hp_n(e): return e + 3
        def b_n(e): return e + 3

        def fused_w(w, part):
            return cT[:, part, w * 2048:(w + 1) * 2048].rearrange("p (k n) -> p k n", k=KC)

        block = ctx.enter_context(nc.Block())

        @block.sync
        def _(sp):
            for k in range(KC):
                for o in range(2):
                    sp.dma_start(fuse_raw[0][o][:, k * V:(k + 1) * V], fuse_in[0, o, :, k * V:(k + 1) * V]).then_inc(chunk_loaded[k], 16)
            for n in range(1, 2 * LAYERS):
                if n >= 2:
                    sp.wait_ge(fuse_lo, fuse_n(n - 2))
                for o in range(2):
                    sp.dma_start(fuse_raw[n % 2][o], fuse_in[n, o]).then_inc(fuse_loaded[n][o], 16)
                if n == 1:
                    sp.dma_start(bias[:, :, :], bias_in).then_inc(consts_in, 16)
                    sp.dma_start(codes_i[:, :], codes_in).then_inc(consts_in, 16)
                    sp.dma_start(roles[:, :], role_in).then_inc(consts_in, 16)
            for b in range(NTB):
                sp.dma_start(x[:, :, b * TB:(b + 1) * TB], x_in[0, b]).then_inc(x_loaded[b], 16)
            for q in range(KC * 2 * LAYERS):
                sp.wait_ge(fuse_copied, q + 1)
                sp.dma_start(fused[q // KC, :, (q % KC) * V:(q % KC + 1) * V], stage[q % KC]).then_inc(fuse_stored[q % KC], 16)
            for s in range(KC):
                sp.wait_ge(fuse_stored[s], 16 * 2 * LAYERS)
            sp.wait_ge(consts_in, 48)

            def load_job(job, src, n):
                sp.wait_ge(w_lo, job)
                sp.dma_start(raw[:, 0:n], src).then_inc(raw_loaded, 16)

            def load_role(layer, half, i, cols, loaded):
                sp.nop(nofuse=True)
                for b in range(2):
                    r = sp.value_load(roles[0:1, bass.ds(half * NB + 2 * i + b, 1)], min_val=0, max_val=ROLES - 1)
                    sp.dma_start(rolep[b * SEQ:(b + 1) * SEQ, i % 2, cols],
                                 roles_in[layer, bass.ds(r, 1), cols].to_broadcast([SEQ, cols.stop - cols.start])).then_inc(loaded[i % 2], 16)

            with sp.Fori(0, HALVES) as half:
                for layer in range(LAYERS):
                    p = 2 * half + layer

                    def load_bd(i):
                        sp.wait_ge(hp_done, hp_n(8 * p + i - 2))
                        load_role(layer, half, i, slice(0, BN), bd_loaded)

                    def load_gb(i):
                        sp.wait_ge(b_done, b_n(8 * p + i - 2))
                        load_role(layer, half, i, slice(BN, RP), gb_loaded)

                    def store(i):
                        if layer == 1:
                            sp.wait_ge(b_done, b_n(8 * p + i))
                            sp.dma_start(out[bass.ds(half * T + i * P, P), :], y[i % 4]).then_inc(stored[i % 4], 16)

                    def next_x(b):
                        if layer == 1:
                            sp.wait_ge(xc_done, 8 * p + TPB * (b + 1))
                            sp.nop(nofuse=True)
                            with sp.If(half < HALVES - 1):
                                sp.dma_start(x[:, :, b * TB:(b + 1) * TB], x_in[1, b]).then_inc(x_loaded[b], 16)

                    load_job(job_c(p, 0), c_in[layer, 0], UP_C + DN)
                    with sp.Fori(1, NG) as g:
                        load_job(job_c(p, g), c_in[layer, bass.ds(g, 1)].rearrange("o p n -> p (o n)"), UP_C + DN)
                    sp.wait_ge(a_lo, 8 * (p + 1))
                    sp.nop(nofuse=True)
                    for i in range(2):
                        load_bd(i)
                        load_gb(i)
                    with sp.Fori(0, NG) as g:
                        load_job(job_m(p, g), m_in[layer, bass.ds(g, 1)].rearrange("o p n -> p (o n)"), LOT)
                    load_job(job_d(p), down_in[layer], LOT)
                    load_job(job_u(p), up_in[layer], LOT)
                    nxt = 2 * layer
                    load_bd(2)
                    load_bd(3)
                    load_job(job_qk(p + 1), fused[nxt], 2048)
                    load_bd(4)
                    for i in range(TILES):
                        if i < TILES - 2:
                            load_gb(i + 2)
                        store(i)
                        if i < TILES - 5:
                            load_bd(i + 5)
                        if i == 1:
                            load_job(job_vp(p + 1), fused[nxt + 1], 2048)
                        if i in (3, 5):
                            next_x(i // 4)
            for s in range(4):
                sp.wait_ge(stored[s], 16 * HALVES * TILES // 4)

        @block.gpsimd
        def _(pool):
            nc.gpsimd.memset(ident[:, :], 0.0).then_inc(made, 1)
            nc.gpsimd.iota(feat[:, :], [[P, KC]], base=0, channel_multiplier=1,
                           allow_small_or_imprecise_dtypes=True).then_inc(made, 1)
            nc.gpsimd.memset(mhalf[:, :], -0.5).then_inc(made, 1)
            pool.wait_ge(made, 1)
            nc.gpsimd.affine_select(out=ident[:, :], in_=ident[:, :], compare_op=ALU.not_equal, fill=1.0,
                                    base=0, pattern=[[-1, P]], channel_multiplier=1).then_inc(made, 1)
            for s in range(2):
                for a, free in ((HI, hp_done), (LO, b_done)):
                    nc.gpsimd.memset(hz[:, s, a, :, 1, :].bitcast(F32), 0.0).then_inc(free, 1)

            with pool.Fori(0, HALVES) as half:
                for layer in range(LAYERS):
                    p = 2 * half + layer
                    pool.wait_ge(xs_lo, 2 * KC * p + 1)
                    pool.wait_ge(oh_ready, LAYERS * KC)
                    pool.nop(nofuse=True)
                    nc.gpsimd.memset(pblk, 0.0).then_inc(p_zeroed, 1)
                    if layer == 1:
                        pool.wait_ge(t3_done, 8 * (half + 1))
                    for k in range(KC):
                        nc.gpsimd.tensor_copy(accv[:, k, :].rearrange("p (b t) -> p b t", b=NB),
                                              oh[:, layer, k, bass.ds(half * NB, NB)].unsqueeze(2).to_broadcast([P, NB, SEQ])
                                              ).then_inc(acc_init, 1)
                    for s in range(2):
                        pool.wait_ge(dn_done, 128 * p + 124 + 4 * s)
                        pool.nop(nofuse=True)
                        nc.gpsimd.memset(hs[:, s, :, :, :].rearrange("p l m (k b t) -> p (l m k) b t", k=2, b=4)[:, :, 1, :].bitcast(F32), 0.0).then_inc(xz_zeroed, 1)
                    with pool.Fori(0, TILES // 4) as four:
                        for i in range(4):
                            e, s = 8 * p + 4 * four + i, i % 2
                            pool.wait_ge(ve_done, e + 1)
                            nc.gpsimd.tensor_tensor(rstd[:, s, :], veps[:, s, :], mhalf[:, :], ALU.pow).then_inc(rstd_done, 1)
                            pool.wait_ge(gb_loaded[s], 32 * (4 * p + 2 * four + i // 2 + 1))
                            pool.wait_ge(yn_done, e + 1)
                            nc.gpsimd.tensor_tensor(y[i], y[i], rolep[:, s, BN + V:BN + 2 * V], ALU.mult).then_inc(g_done, 1)
                            pool.wait_ge(g_done, e + 1)
                            nc.gpsimd.tensor_tensor(y[i], y[i], rolep[:, s, BN + 2 * V:BN + 3 * V], ALU.add).then_inc(b_done, 1)
                    if layer == 1:
                        for s in range(4):
                            pool.wait_ge(stored[s], 16 * (TILES // 4) * (half + 1))

        @block.tensor
        def _(pe):
            pe.wait_ge(made, 4)

            def product(out, pairs, start=True, stop=True):
                n, total = 0, 3 * len(pairs)
                for lhs, rhs, wait in pairs:
                    if wait is not None:
                        pe.wait_ge(*wait)
                    for a, b in PRODUCTS:
                        mm = nc.tensor.matmul(out, lhs(a), rhs(b), start=(start and n == 0), stop=(stop and n == total - 1))
                        n += 1
                return mm

            for k in range(KC):
                pe.wait_ge(fuse_lo, 2 * (k + 1))
                u, w = fuse_parts[0]
                for c in range(KC):
                    mm = product(fuse_bank[0][c][:, :], [(lambda a: u[:, a, k * V + c * P:k * V + (c + 1) * P],
                                                          lambda a: w[:, a, k * V:(k + 1) * V], None)], k == 0, k == KC - 1)
                    if k == KC - 1:
                        mm.then_inc(fuse_mm, 1)
            for n in range(1, 2 * LAYERS):
                pe.wait_ge(fuse_lo, fuse_n(n))
                u, w = fuse_parts[n % 2]
                for c in range(KC):
                    if n >= 2:
                        pe.wait_ge(fuse_copied, KC * (n - 2) + c + 1)
                    product(fuse_bank[n % 2][c][:, :], [
                        (lambda a, k=k: u[:, a, k * V + c * P:k * V + (c + 1) * P], lambda a, k=k: w[:, a, k * V:(k + 1) * V], None)
                        for k in range(KC)]).then_inc(fuse_mm, 1)
            pe.wait_ge(consts_in, 48)

            def attention(p, half, layer, b):
                cols = slice(b * TB, (b + 1) * TB)
                if b == 0:
                    pe.wait_ge(w_lo, job_qk(p) + 1)
                for j in range(KC):
                    if b == 0 and j == 2:
                        pe.wait_ge(w_lo, job_vp(p) + 1)
                    if b == 0 and layer == 1 and j in (1, 2):
                        pe.wait_ge(x_back, 8 * half + 4 + j)
                    if b == 1:
                        pe.wait_ge(a_sum, 16 * p + j + 1)
                    product(t_bank[j][:, :], [
                        (lambda a, k=k: fused_w(0, a)[:, k, j * P:(j + 1) * P], lambda c, k=k: aT[:, c, k, cols],
                         (xs_lo, 8 * p + KC * b + k + 1) if j == 0 else None) for k in range(KC)]).then_inc(t_done, 1)
                    if b == 0 and layer == 1 and j % 2:
                        turn_back(p - 1, half, TILES - 2 + j // 2)
                if b == 0:
                    pe.wait_ge(t_lo, 8 * p + 1)

                def values(i):
                    if b == 1 and i < 2:
                        pe.wait_ge(a_sum, 16 * p + 4 + i + 1)
                    if i >= 2:
                        pe.wait_ge(v_lo, 8 * p + TPB * b + i - 1)
                    product(v_bank[i % 2][:, :], [
                        (lambda a, k=k: aT[:, a, k, b * TB + i * P:b * TB + (i + 1) * P], lambda c, k=k: fused_w(1, c)[:, k, :], None)
                        for k in range(KC)]).then_inc(v_done, 1)

                def all_scores():
                    if b == 1:
                        pe.wait_ge(a_sum, 16 * p + 8)
                    elif layer == 1:
                        pe.wait_ge(x_back, 8 * (half + 1))
                    for i in range(TPB):
                        out = s_bank[i // 2][:, (i % 2) * 256:(i % 2 + 1) * 256]
                        tile = slice(b * TB + i * P, b * TB + (i + 1) * P)
                        for j in range(KC):
                            if i == 0:
                                pe.wait_ge(t_lo, 8 * p + KC * b + j + 1)
                            nc.tensor.matmul(out, hs[:, j // 2, HI, j % 2, i * P:(i + 1) * P], aT[:, :, j, tile],
                                             start=(j == 0), stop=False)
                            mm = nc.tensor.matmul(out[:, 0:P], hs[:, j // 2, LO, j % 2, i * P:(i + 1) * P], aT[:, HI, j, tile],
                                                  start=False, stop=(j == KC - 1))
                    mm.then_inc(s_done, 1)

                values(0)
                all_scores()
                values(1)
                values(2)
                pe.wait_ge(p_ready, 4 * p + 2 * b + 2)
                for i in range(TPB):
                    mm = nc.tensor.transpose(pt_bank[:, i * P:(i + 1) * P], pblk[:, i, :], ident[:, :])
                mm.then_inc(pt_done, 1)
                values(3)
                pe.wait_ge(pt_lo, 2 * p + b + 1)
                for pair in range(2):
                    pe.wait_ge(v_lo, 8 * p + TPB * b + 2 * pair + 2)
                    for f in range(KC):
                        for i in range(2 * pair, 2 * pair + 2):
                            out = a_bank[pair][f][:, (i % 2) * 256:(i % 2 + 1) * 256]
                            v_cols, p_cols = slice(i * V + f * P, i * V + (f + 1) * P), slice(2048 + i * P, 2048 + (i + 1) * P)
                            nc.tensor.matmul(out, slot[1][:, HI, v_cols], slot[1][:, :, p_cols], start=True, stop=False)
                            mm = nc.tensor.matmul(out[:, 0:P], slot[1][:, LO, v_cols], slot[1][:, HI, p_cols], start=False, stop=True)
                        mm.then_inc(pv_done, 1)

            def up(p, r, kind, g_job, s, b):
                kin = KC * (1 + kind)
                if b == 0:
                    pe.wait_ge(w_lo, g_job + 1)
                for m in range(MC):
                    if kind == 0 and isinstance(r, int) and r == 0:
                        pe.wait_ge(a_sum, 16 * p + 12 + m + 1)
                    else:
                        pe.wait_ge(h_hi, 64 * p + 2 * (r - 1) + m + 1)
                    pairs = []
                    for k in range(kin):
                        src = aT if k < KC else cTv
                        wait = None
                        if m == 0 and kind == 0 and k == 0:
                            wait = (a_lo, 8 * p + KC * (b + 1))
                        if m == 0 and kind == 1 and k >= KC:
                            wait = (c_lo, 8 * p + KC * b + k - KC + 1)
                        pairs.append((lambda a, k=k: slot[s][:, a, k * GH + m * P:k * GH + (m + 1) * P],
                                      lambda c, k=k, src=src: src[:, c, k % KC, b * TB:(b + 1) * TB], wait))
                    product(ps[m][:, :], pairs).then_inc(up_done, 1)

            def down(p, r, kind, s, b):
                base = UP_M if kind else UP_C
                for o in range(KC):
                    if not (kind == 0 and isinstance(r, int) and r == 0):
                        pe.wait_ge(acc_done, 128 * p + 4 * (r - 1) + o + 1)
                    product(ps[2 + o][:, :], [
                        (lambda a, m=m: slot[s][:, a, base + m * V + o * P:base + m * V + (o + 1) * P],
                         lambda c, m=m: hs[:, b, c, m, :],
                         (h_lo, 64 * p + 2 * r + m + 1) if o == 0 else None) for m in range(MC)]).then_inc(dn_done, 1)

            def mlp(p, kind):
                job = job_m if kind else job_c
                first = STEPS * kind
                up(p, first, kind, job(p, 0), 0, 0)

                def four(g0, last):
                    for t in range(4):
                        r = first + 2 * g0 + t
                        if not (last and t == 3):
                            n = t + 1
                            up(p, r + 1, kind, job(p, g0 + n // 2), (n // 2) % 2, n % 2)
                        down(p, r, kind, (t // 2) % 2, t % 2)

                if kind == 0:
                    four(0, False)
                    with pe.Fori(1, NG // 2 - 1) as gp:
                        four(2 * gp, False)
                else:
                    with pe.Fori(0, NG // 2 - 1) as gp:
                        four(2 * gp, False)
                four(NG - 2, True)

            def tile_roles(half, i):
                pe.nop(nofuse=True)
                return [pe.value_load(roles[0:1, bass.ds(half * NB + 2 * i + b, 1)], min_val=0, max_val=ROLES - 1)
                        for b in range(2)]

            def front(p, half, i):
                e, s = 8 * p + i, i % 2
                r = tile_roles(half, i)
                if i == 0:
                    pe.wait_ge(w_lo, job_d(p) + 1)
                if i < 2:
                    pe.wait_ge(xz_zeroed, 2 * p + i + 1)
                else:
                    pe.wait_ge(hp_done, hp_n(e - 2))
                pe.wait_ge(xz_lo, e + 1)
                n = 0
                for b in range(2):
                    for k in range(KC):
                        for a, c in PRODUCTS:
                            mm = nc.tensor.matmul(d_bank[s][:, 0:BN], xz[s][:, a, k, b:b + 2, :],
                                                  slot[0][:, c, bass.ds(r[b] * (KC * BN) + k * BN, BN)],
                                                  start=(n == 0), stop=(n == 6 * KC - 1))
                            n += 1
                mm.then_inc(d_done, 1)
                if i >= 3:
                    pe.wait_ge(y_done, e - 2)
                for k in range(KC):
                    mm = nc.tensor.matmul(u_bank[i % 3][:, k * P:(k + 1) * P], xc[s][:, k, :], ident[:, :], start=(k == 0), stop=False)
                mm.then_inc(t1_done, 1)
                return r

            def turn_h(p, i):
                e, s = 8 * p + i, i % 2
                pe.wait_ge(hg_done, e + 1)
                if i == 0:
                    pe.wait_ge(acc_done, 128 * p + 128)
                else:
                    pe.wait_ge(hz_lo, e)
                for k in range(2):
                    mm = nc.tensor.transpose(h_bank[:, k * P:(k + 1) * P], hg[s][:, k * P:(k + 1) * P], ident[:, :])
                mm.then_inc(t2_done, 1)

            def adapter_up(p, i, r):
                e, s = 8 * p + i, i % 2
                if i == 0:
                    pe.wait_ge(w_lo, job_u(p) + 1)
                pe.wait_ge(hz_lo, e + 1)
                n = 0
                for b in range(2):
                    for k in range(2):
                        for a, c in PRODUCTS:
                            mm = nc.tensor.matmul(u_bank[i % 3][:, :], hz[:, s, a, k, b:b + 2, :],
                                                  slot[1][:, c, bass.ds(r[b] * (2 * V) + k * V, V)],
                                                  start=False, stop=(n == 11))
                            n += 1
                mm.then_inc(u_done, 1)

            def turn_back(p, half, i):
                pe.wait_ge(b_done, b_n(8 * p + i))
                if 2 <= i < TILES - 2:
                    pe.wait_ge(x_back, 8 * half + i - 1)
                for k in range(KC):
                    mm = nc.tensor.transpose(back_bank[i][:, k * P:(k + 1) * P], y[i % 4][:, k * P:(k + 1) * P], ident[:, :])
                mm.then_inc(t3_done, 1)

            with pe.Fori(0, HALVES) as half:
                for layer in range(LAYERS):
                    p = 2 * half + layer
                    for b in range(NTB):
                        attention(p, half, layer, b)
                    mlp(p, 0)
                    mlp(p, 1)
                    r = {i: front(p, half, i) for i in range(2)}
                    turn_h(p, 0)
                    for i in range(TILES):
                        if i + 2 < TILES:
                            r[i + 2] = front(p, half, i + 2)
                        if i + 1 < TILES:
                            turn_h(p, i + 1)
                        if layer == 0 and 2 <= i < TILES - 1:
                            turn_back(p, half, i - 2)
                        adapter_up(p, i, r.pop(i))
                    if layer == 0:
                        turn_back(p, half, TILES - 3)

        @block.scalar
        def _(act):
            def split_hi(job, n, dst, *free):
                act.wait_ge(raw_loaded, 16 * (job - 1))
                for w in free:
                    act.wait_ge(*w)
                nc.scalar.activation(dst, raw[:, 0:n], ACT.Copy).then_inc(w_hi, 1)

            def operands(n):
                if n == 0:
                    for k in range(KC):
                        act.wait_ge(chunk_loaded[k], 32)
                        for o in range(2):
                            cols = slice(k * V, (k + 1) * V)
                            nc.scalar.activation(fuse_parts[0][o][:, HI, cols], fuse_raw[0][o][:, cols], ACT.Copy).then_inc(fuse_hi, 1)
                    return
                if n >= 2:
                    act.wait_ge(fuse_mm, KC * (n - 1))
                for o in range(2):
                    act.wait_ge(fuse_loaded[n][o], 16)
                    nc.scalar.activation(fuse_parts[n % 2][o][:, HI, :], fuse_raw[n % 2][o], ACT.Copy).then_inc(fuse_hi, 1)

            def results(n):
                for c in range(KC):
                    q = KC * n + c
                    act.wait_ge(fuse_mm, q + 1)
                    if n >= 2:
                        nc.scalar.activation(cT[:, HI, 2048 * (n - 2) + c * V:2048 * (n - 2) + (c + 1) * V],
                                             fuse_bank[n % 2][c][:, :], ACT.Copy)
                    if n >= 1:
                        act.wait_ge(fuse_stored[c], 16 * n)
                    nc.scalar.activation(stage[c], fuse_bank[n % 2][c][:, :], ACT.Copy).then_inc(fuse_copied, 1)

            def split_block(p, half, layer, b, k):
                if layer == 0:
                    act.wait_ge(x_loaded[b], 16 * (half + 1))
                else:
                    act.wait_ge(x_back, 8 * half + TPB * (b + 1))
                cols = slice(b * TB, (b + 1) * TB)
                nc.scalar.activation(aT[:, HI, k, cols], x[:, k, cols], ACT.Copy).then_inc(xs_hi, 1)

            for n in range(3):
                operands(n)
            results(0)
            operands(3)
            results(1)
            results(2)
            for k in range(KC):
                split_block(0, 0, 0, 0, k)
            results(3)
            act.wait_ge(consts_in, 48)

            def back(half, i):
                act.wait_ge(t3_done, 8 * half + i + 1)
                nc.scalar.activation(x[:, :, i * P:(i + 1) * P], back_bank[i][:, :].rearrange("p (k t) -> p k t", k=KC),
                                     ACT.Copy).then_inc(x_back, 1)

            def attention(p, half, layer, b):
                cols = slice(b * TB, (b + 1) * TB)
                for j in range(KC):
                    act.wait_ge(t_done, 8 * p + KC * b + j + 1)
                    nc.scalar.activation(hs[:, j // 2, HI, j % 2, :], t_bank[j][:, :], ACT.Copy).then_inc(t_hi, 1)
                    if b == 0 and layer == 1 and j % 2:
                        back(half, TILES - 2 + j // 2)

                def values(i):
                    act.wait_ge(v_done, 8 * p + TPB * b + i + 1)
                    nc.scalar.activation(slot[1][:, HI, i * V:(i + 1) * V], v_bank[i % 2][:, :], ACT.Copy).then_inc(v_hi, 1)

                values(0)
                if b == 0:
                    for k in range(KC):
                        split_block(p, half, layer, 1, k)
                act.wait_ge(s_done, 2 * p + b + 1)
                for h in range(2):
                    nc.scalar.activation(ex[batch_rows[h], :, :], diagonal(h, 1), ACT.Copy).then_inc(s_half, 1)
                act.wait_ge(sm_ready, 2 * p + b + 1)
                nc.scalar.activation(ex, sm, ACT.Exp, scale=SCALE).then_inc(ex_done, 1)
                values(1)
                values(2)
                act.wait_ge(pt_done, 2 * p + b + 1)
                nc.scalar.activation(slot[1][:, HI, 2048:2560], pt_bank[:, :], ACT.Copy).then_inc(pt_hi, 1)
                values(3)
                for pair in range(2):
                    for f in range(KC):
                        act.wait_ge(pv_done, 16 * p + 8 * b + 4 * pair + f + 1)
                        nc.scalar.activation(a_pair[pair][f], a_halves(pair, f)[:, :, 1, :], ACT.Identity,
                                             bias=bias[:, layer, BP + f:BP + f + 1]).then_inc(a_half, 1)
                for f in range(KC):
                    act.wait_ge(a_sum, 16 * p + 8 * b + 4 + f + 1)
                    nc.scalar.activation(aT[:, HI, f, cols], a_out[:, f, :], ACT.Copy).then_inc(a_hi, 1)
                if b == 0:
                    split_hi(job_c(p, 0), UP_C + DN, slot[0][:, HI, 0:UP_C + DN])

            def hidden(p, layer, kind, r, g, b):
                for m in range(MC):
                    act.wait_ge(up_done, 64 * p + 2 * r + m + 1)
                    early = kind == 0 and isinstance(r, int)
                    if not (early and r == 0):
                        act.wait_ge(h_lo, 64 * p + 2 * (r - 1) + m + 1)
                    if not (early and r < 2):
                        act.wait_ge(dn_done, 128 * p + 4 * (r - 1))
                    col = (MB1 if kind else CB1) + MC * g + m
                    b1 = bias[:, layer, bass.ds(col, 1)]
                    act.nop(nofuse=True)
                    nc.scalar.activation(hraw[:, m, :], ps[m][:, :], ACT.Gelu, bias=b1)
                    nc.scalar.activation(hs[:, b, HI, m, :], ps[m][:, :], ACT.Gelu, bias=b1).then_inc(h_hi, 1)

            def mlp(p, layer, kind):
                n = LOT if kind else UP_C + DN
                job = job_m if kind else job_c
                first = STEPS * kind

                def group(g, s, nxt, first_c=False):
                    r = first + 2 * g
                    hidden(p, layer, kind, r, g, 0)
                    if nxt:
                        free = (pv_done, 16 * p + 16) if first_c else (dn_done, 128 * p + 4 * r)
                        split_hi(job(p, g + 1), n, slot[1 - s][:, HI, 0:n], free)
                    elif kind == 0:
                        split_hi(job_m(p, 0), LOT, slot[0][:, HI, 0:LOT], (dn_done, 128 * p + 4 * r))
                    else:
                        split_hi(job_d(p), LOT, slot[0][:, HI, 0:LOT], (dn_done, 128 * p + 4 * r))
                    hidden(p, layer, kind, r + 1, g, 1)

                if kind == 0:
                    group(0, 0, True, True)
                    group(1, 1, True)
                    with act.Fori(1, NG // 2 - 1) as gp:
                        group(2 * gp, 0, True)
                        group(2 * gp + 1, 1, True)
                else:
                    with act.Fori(0, NG // 2 - 1) as gp:
                        group(2 * gp, 0, True)
                        group(2 * gp + 1, 1, True)
                group(NG - 2, 0, True)
                group(NG - 1, 1, False)

            with act.Fori(0, HALVES) as half:
                for layer in range(LAYERS):
                    p = 2 * half + layer
                    for b in range(NTB):
                        attention(p, half, layer, b)
                    mlp(p, layer, 0)
                    for b in range(NTB):
                        for o in range(KC):
                            act.wait_ge(acc_done, 128 * p + 4 * (STEPS - 2 + b) + o + 1)
                            nc.scalar.activation(cTv[:, HI, o, b * TB:(b + 1) * TB], accv[:, o, b * TB:(b + 1) * TB],
                                                 ACT.Copy).then_inc(c_hi, 1)
                    mlp(p, layer, 1)

                    def split_x(i):
                        e, s = 8 * p + i, i % 2
                        act.wait_ge(xc_done, e + 1)
                        if i < 2:
                            act.wait_ge(dn_done, 128 * p + 124 + 4 * i)
                        else:
                            act.wait_ge(d_done, e - 1)
                        nc.scalar.activation(xz[s][:, HI, :, 0:3:2, :], xc[s].rearrange("p k (b t) -> p k b t", b=2),
                                             ACT.Copy).then_inc(xz_hi, 1)

                    def gelu_h(i):
                        act.wait_ge(hp_done, hp_n(8 * p + i))
                        nc.scalar.activation(hg[i % 2], hp[i % 2], ACT.Gelu).then_inc(hg_done, 1)

                    def split_h(i):
                        act.wait_ge(t2_done, 8 * p + i + 1)
                        nc.scalar.activation(hz[:, i % 2, HI, :, 0:3:2, :], h_bank[:, 0:BN].rearrange("p (k b t) -> p k b t", k=2, b=2),
                                             ACT.Copy).then_inc(hz_hi, 1)

                    def fused_hi_part(q):
                        act.wait_ge(raw_loaded, 16 * (job_qk(p + 1) + q // 2 - 1))
                        nc.scalar.activation(cT[:, HI, 1024 * q:1024 * (q + 1)], raw[:, 1024 * (q % 2):1024 * (q % 2 + 1)],
                                             ACT.Copy).then_inc(w_hi if q % 2 else fused_hi, 1)

                    split_x(0)
                    split_x(1)
                    split_hi(job_u(p), LOT, slot[1][:, HI, 0:LOT])
                    gelu_h(0)
                    split_x(2)
                    gelu_h(1)
                    split_h(0)
                    for i in range(TILES):
                        if i + 3 < TILES:
                            split_x(i + 3)
                        if i + 2 < TILES:
                            gelu_h(i + 2)
                        if i + 1 < TILES:
                            split_h(i + 1)
                        if layer == 0 and 2 <= i < TILES - 1:
                            back(half, i - 2)
                        if i in fused_hi_steps:
                            fused_hi_part(fused_hi_steps[i])
                        if i == TILES - 2:
                            if layer == 0:
                                for k in range(KC):
                                    split_block(p + 1, half, 1, 0, k)
                            else:
                                act.nop(nofuse=True)
                                with act.If(half < HALVES - 1):
                                    for k in range(KC):
                                        split_block(p + 1, half + 1, 0, 0, k)
                    if layer == 0:
                        back(half, TILES - 3)

        @block.vector
        def _(dve):
            def minus(out, a, hi):
                return nc.vector.tensor_tensor(out, a, hi.bitcast(F32), ALU.subtract)

            def split_lo(job, n, dst):
                dve.wait_ge(w_hi, job - 1)
                minus(dst[:, LO, :], raw[:, 0:n], dst[:, HI, :]).then_inc(w_lo, 1)

            def operands(n):
                if n == 0:
                    for k in range(KC):
                        for o in range(2):
                            dve.wait_ge(fuse_hi, 2 * k + o + 1)
                            u, cols = fuse_parts[0][o], slice(k * V, (k + 1) * V)
                            minus(u[:, LO, cols], fuse_raw[0][o][:, cols], u[:, HI, cols]).then_inc(fuse_lo, 1)
                    return
                for o in range(2):
                    dve.wait_ge(fuse_hi, fuse_n(n) - 1 + o)
                    u = fuse_parts[n % 2][o]
                    minus(u[:, LO, :], fuse_raw[n % 2][o], u[:, HI, :]).then_inc(fuse_lo, 1)

            def results(n):
                for c in range(KC):
                    dve.wait_ge(fuse_copied, KC * n + c + 1)
                    cols = slice(2048 * (n - 2) + c * V, 2048 * (n - 2) + (c + 1) * V)
                    mm = minus(cT[:, LO, cols], fuse_bank[n % 2][c][:, :], cT[:, HI, cols])
                    mm.then_inc(w_lo if c == KC - 1 else fused_lo, 1)

            operands(0)
            operands(1)
            dve.wait_ge(consts_in, 48)
            nc.vector.tensor_copy(codes[:, :], codes_i[:, :]).then_inc(codes_ready, 1)
            dve.wait_ge(codes_ready, 1)
            dve.wait_ge(made, 4)
            for layer in range(LAYERS):
                for k in range(KC):
                    nc.vector.tensor_scalar(oh[:, layer, k, :], codes[:, :], feat[:, k:k + 1],
                                            bias[:, layer, CB2 + k:CB2 + k + 1], ALU.is_equal, ALU.add).then_inc(oh_ready, 1)
            operands(2)
            operands(3)
            results(2)

            def split_block(p, b, k):
                dve.wait_ge(xs_hi, 8 * p + KC * b + k + 1)
                cols = slice(b * TB, (b + 1) * TB)
                minus(aT[:, LO, k, cols], x[:, k, cols], aT[:, HI, k, cols]).then_inc(xs_lo, 1)

            for k in range(KC):
                split_block(0, 0, k)
            results(3)

            def attention(p, layer, b):
                cols = slice(b * TB, (b + 1) * TB)
                for j in range(KC):
                    dve.wait_ge(t_hi, 8 * p + KC * b + j + 1)
                    minus(hs[:, j // 2, LO, j % 2, :], t_bank[j][:, :], hs[:, j // 2, HI, j % 2, :]).then_inc(t_lo, 1)
                def values(i):
                    dve.wait_ge(v_hi, 8 * p + TPB * b + i + 1)
                    minus(slot[1][:, LO, i * V:(i + 1) * V], v_bank[i % 2][:, :], slot[1][:, HI, i * V:(i + 1) * V]).then_inc(v_lo, 1)

                values(0)
                if b == 0:
                    for k in range(KC):
                        split_block(p, 1, k)
                rows = batch_rows
                for h in range(2):
                    dve.wait_ge(s_half, 4 * p + 2 * b + h + 1)
                    nc.vector.tensor_tensor(sm[rows[h], :, :], diagonal(h, 0), ex[rows[h], :, :], ALU.add).then_inc(ss_done, 1)
                dve.wait_ge(ss_done, 4 * p + 2 * b + 2)
                nc.vector.tensor_reduce(mx[:, :], sm, AX_X, ALU.max).then_inc(mx_done, 1)
                dve.wait_ge(mx_done, 2 * p + b + 1)
                nc.vector.tensor_tensor(sm, sm, mx[:, :].unsqueeze(2).to_broadcast([P, TPB, SEQ]), ALU.subtract).then_inc(sm_ready, 1)
                dve.wait_ge(ex_done, 2 * p + b + 1)
                nc.vector.tensor_reduce(rsum[:, :], ex, AX_X, ALU.add).then_inc(rs_done, 1)
                dve.wait_ge(rs_done, 2 * p + b + 1)
                nc.vector.reciprocal(rinv[:, :], rsum[:, :]).then_inc(ri_done, 1)
                dve.wait_ge(ri_done, 2 * p + b + 1)
                dve.wait_ge(p_zeroed, p + 1)
                for h in range(2):
                    nc.vector.tensor_tensor(pblk[rows[h], :, h * SEQ:(h + 1) * SEQ], ex[rows[h], :, :],
                                            rinv[rows[h], :].unsqueeze(2).to_broadcast([SEQ, TPB, SEQ]), ALU.mult).then_inc(p_ready, 1)
                values(1)
                values(2)
                dve.wait_ge(pt_hi, 2 * p + b + 1)
                minus(slot[1][:, LO, 2048:2560], pt_bank[:, :], slot[1][:, HI, 2048:2560]).then_inc(pt_lo, 1)
                values(3)
                for pair in range(2):
                    for f in range(KC):
                        dve.wait_ge(a_half, 16 * p + 8 * b + 4 * pair + f + 1)
                        nc.vector.tensor_tensor(a_pair[pair][f], a_halves(pair, f)[:, :, 0, :], a_pair[pair][f], ALU.add).then_inc(a_sum, 1)
                for f in range(KC):
                    dve.wait_ge(a_hi, 8 * p + KC * b + f + 1)
                    minus(aT[:, LO, f, cols], a_out[:, f, :], aT[:, HI, f, cols]).then_inc(a_lo, 1)
                if b == 0:
                    split_lo(job_c(p, 0), UP_C + DN, slot[0][:, :, 0:UP_C + DN])

            def hidden(p, r, b):
                for m in range(MC):
                    dve.wait_ge(h_hi, 64 * p + 2 * r + m + 1)
                    minus(hs[:, b, LO, m, :], hraw[:, m, :], hs[:, b, HI, m, :]).then_inc(h_lo, 1)

            def add(p, kind, r, b):
                for o in range(KC):
                    dve.wait_ge(dn_done, 128 * p + 4 * r + o + 1)
                    dst = (x[:, o, :] if kind else accv[:, o, :])[:, b * TB:(b + 1) * TB]
                    nc.vector.tensor_tensor(dst, ps[2 + o][:, :], dst, ALU.add).then_inc(acc_done, 1)

            def mlp(p, kind):
                n = LOT if kind else UP_C + DN
                job = job_m if kind else job_c
                first = STEPS * kind
                hidden(p, first, 0)

                def group(g, s, nxt):
                    r = first + 2 * g
                    if nxt:
                        split_lo(job(p, g + 1), n, slot[1 - s][:, :, 0:n])
                    elif kind == 0:
                        split_lo(job_m(p, 0), LOT, slot[0][:, :, 0:LOT])
                    else:
                        split_lo(job_d(p), LOT, slot[0][:, :, 0:LOT])
                    hidden(p, r + 1, 1)
                    add(p, kind, r, 0)
                    if nxt:
                        hidden(p, r + 2, 0)
                        add(p, kind, r + 1, 1)

                with dve.Fori(0, NG // 2 - 1) as gp:
                    group(2 * gp, 0, True)
                    group(2 * gp + 1, 1, True)
                group(NG - 2, 0, True)
                group(NG - 1, 1, False)

            with dve.Fori(0, HALVES) as half:
                for layer in range(LAYERS):
                    p = 2 * half + layer
                    for b in range(NTB):
                        attention(p, layer, b)
                    dve.wait_ge(acc_init, KC * (p + 1))
                    mlp(p, 0)
                    for b in range(NTB):
                        cols = slice(b * TB, (b + 1) * TB)
                        if b == 1:
                            add(p, 0, STEPS - 1, 1)
                        for o in range(KC):
                            dve.wait_ge(acc_done, 128 * p + 4 * (STEPS - 2 + b) + o + 1)
                            nc.vector.scalar_tensor_tensor(out=x[:, o, cols], in0=accv[:, o, cols], scalar=bias[:, layer, MB2 + o:MB2 + o + 1],
                                                           in1=x[:, o, cols], op0=ALU.add, op1=ALU.add)
                            dve.wait_ge(c_hi, 8 * p + KC * b + o + 1)
                            minus(cTv[:, LO, o, cols], accv[:, o, cols], cTv[:, HI, o, cols]).then_inc(c_lo, 1)
                    mlp(p, 1)

                    def clip(i):
                        if i >= 2:
                            dve.wait_ge(t1_done, 8 * p + i - 1)
                        nc.vector.tensor_scalar(xc[i % 2], x[:, :, i * P:(i + 1) * P], 0.0, 1.0, ALU.max, ALU.min).then_inc(xc_done, 1)

                    def split_x(i):
                        s = i % 2
                        dve.wait_ge(xz_hi, 8 * p + i + 1)
                        minus(xz[s][:, LO, :, 0:3:2, :], xc[s].rearrange("p k (b t) -> p k b t", b=2), xz[s][:, HI, :, 0:3:2, :]).then_inc(xz_lo, 1)

                    def params(i):
                        return 32 * (4 * p + i // 2 + 1)

                    def h_bias(i):
                        dve.wait_ge(bd_loaded[i % 2], params(i))
                        dve.wait_ge(d_done, 8 * p + i + 1)
                        if i >= 2:
                            dve.wait_ge(hg_done, 8 * p + i - 1)
                        nc.vector.tensor_tensor(hp[i % 2], d_bank[i % 2][:, 0:BN], rolep[:, i % 2, 0:BN], ALU.add).then_inc(hp_done, 1)

                    def split_h(i):
                        s = i % 2
                        dve.wait_ge(hz_hi, 8 * p + i + 1)
                        minus(hz[:, s, LO, :, 0:3:2, :], h_bank[:, 0:BN].rearrange("p (k b t) -> p k b t", k=2, b=2),
                              hz[:, s, HI, :, 0:3:2, :]).then_inc(hz_lo, 1)

                    def row_stats(i):
                        e, s = 8 * p + i, i % 2
                        dve.wait_ge(gb_loaded[s], params(i))
                        dve.wait_ge(u_done, e + 1)
                        rows = y[i % 4]
                        if i >= 4:
                            if layer == 0:
                                dve.wait_ge(t3_done, 8 * half + i - 3)
                            else:
                                dve.wait_ge(stored[i % 4], 16 * (2 * half + i // 4))
                        nc.vector.tensor_tensor(rows, u_bank[i % 3][:, :], rolep[:, s, BN:BN + V], ALU.add).then_inc(y_done, 1)
                        dve.wait_ge(y_done, e + 1)
                        nc.vector.bn_stats(stats[:, s, :], rows).then_inc(st_done, 1)
                        dve.wait_ge(st_done, e + 1)
                        dve.nop(nofuse=True)
                        nc.vector.bn_aggr(mv[:, s, :], stats[:, s, :]).then_inc(ag_done, 1)
                        dve.wait_ge(ag_done, e + 1)
                        nc.vector.tensor_scalar(veps[:, s, :], mv[:, s, 1:2], EPS, None, ALU.add).then_inc(ve_done, 1)

                    def normalise(i):
                        s = i % 2
                        dve.wait_ge(rstd_done, 8 * p + i + 1)
                        nc.vector.tensor_scalar(y[i % 4], y[i % 4], mv[:, s, 0:1], rstd[:, s, :], ALU.subtract, ALU.mult).then_inc(yn_done, 1)

                    def fused_lo_part(q):
                        if q % 2:
                            dve.wait_ge(w_hi, job_qk(p + 1) + q // 2 - 1)
                        else:
                            dve.wait_ge(fused_hi, 2 * p + q // 2 + 1)
                        minus(cT[:, LO, 1024 * q:1024 * (q + 1)], raw[:, 1024 * (q % 2):1024 * (q % 2 + 1)],
                              cT[:, HI, 1024 * q:1024 * (q + 1)]).then_inc(w_lo if q % 2 else fused_lo, 1)

                    dve.wait_ge(acc_done, 128 * p + 124)
                    clip(0)
                    split_x(0)
                    clip(1)
                    add(p, 1, 2 * STEPS - 1, 1)
                    split_x(1)
                    h_bias(0)
                    clip(2)
                    split_x(2)
                    dve.wait_ge(w_hi, job_u(p) - 1)
                    minus(slot[1][:, LO, 0:LOT // 2], raw[:, 0:LOT // 2], slot[1][:, HI, 0:LOT // 2])
                    h_bias(1)
                    split_h(0)
                    minus(slot[1][:, LO, LOT // 2:LOT], raw[:, LOT // 2:LOT], slot[1][:, HI, LOT // 2:LOT]).then_inc(w_lo, 1)
                    for i in range(TILES):
                        if i == TILES - 2:
                            split_h(i + 1)
                        if i >= 1:
                            row_stats(i - 1)
                        if i + 3 < TILES:
                            if i + 3 == TPB:
                                dve.wait_ge(acc_done, 128 * p + 128)
                            clip(i + 3)
                            split_x(i + 3)
                        if i >= 1:
                            normalise(i - 1)
                        if i in fused_lo_steps:
                            fused_lo_part(fused_lo_steps[i])
                        if i + 2 < TILES:
                            h_bias(i + 2)
                        if i + 2 < TILES:
                            split_h(i + 1)
                        if i == TILES - 2:
                            if layer == 0:
                                for k in range(KC):
                                    split_block(p + 1, 0, k)
                            else:
                                dve.nop(nofuse=True)
                                with dve.If(half < HALVES - 1):
                                    for k in range(KC):
                                        split_block(p + 1, 0, k)
                    row_stats(TILES - 1)
                    normalise(TILES - 1)


def _chunks(w):
    import numpy as np
    r, n = w.shape
    return np.ascontiguousarray(w.reshape(r // P, P, n).transpose(1, 0, 2).reshape(P, -1))


def kernel(**inputs):
    import numpy as np
    import concourse.bacc as bacc
    from concourse.bass_utils import run_bass_kernel_spmd

    a = {k: np.asarray(v) for k, v in inputs.items()}
    blocks, adapters = ("L0_cond_", "L2_cond_"), ("L1_cond_", "L3_cond_")
    gains = (("gamma", "beta"), ("ln_w", "ln_b"))

    def groups(w1, w2):
        return np.stack([np.concatenate([_chunks(w1[:, g * GH:(g + 1) * GH]), _chunks(w2[g * GH:(g + 1) * GH])], 1)
                         for g in range(NG)])

    def columns(b):
        return b.reshape(-1, P).T

    arrays = {
        "x_in": np.ascontiguousarray(a["x"].reshape(HALVES, NTB, TB, KC, P).transpose(0, 1, 4, 3, 2)),
        "fuse_in": np.stack([np.stack([_chunks(u), _chunks(w)]) for l in blocks[::-1]
                             for u, w in ((a[l + "Wq"].T, a[l + "Wk"].T), (a[l + "Wv"].T, a[l + "Wp"]))]),
        "c_in": np.stack([groups(a[l + "cW1"], a[l + "cW2"]) for l in blocks]),
        "m_in": np.stack([groups(a[l + "mW1"], a[l + "mW2"]) for l in blocks]),
        "down_in": np.stack([np.concatenate([_chunks(a[l + "W_down"][r]) for r in range(ROLES)], 1) for l in adapters]),
        "up_in": np.stack([np.concatenate([_chunks(a[l + "W_up"][r]) for r in range(ROLES)], 1) for l in adapters]),
        "roles_in": np.stack([np.concatenate([a[l + "b_down"], a[l + "b_up"], a[l + g], a[l + b]], 1)
                              for l, (g, b) in zip(adapters, gains)]),
        "bias_in": np.ascontiguousarray(np.stack([np.concatenate([columns(a[l + n]) for n in ("cb1", "mb1", "bp", "cb2", "mb2")], 1)
                                                  for l in blocks], 1)),
        "codes_in": np.ascontiguousarray(np.broadcast_to(a["itok_B_17_1546"].reshape(1, BATCHES), (P, BATCHES))),
        "role_in": np.ascontiguousarray(a["itok_B_1_2"].reshape(1, BATCHES)),
    }
    nc = bacc.Bacc("TRN2", target_bir_lowering=False, num_devices=1)
    args = [nc.dram_tensor(n, v.shape, mybir.dt.from_np(v.dtype), kind="ExternalInput").ap() for n, v in arrays.items()]
    args.append(nc.dram_tensor("out", (BATCHES * SEQ, V), F32, kind="ExternalOutput").ap())
    cond_seq_kernel(nc, *args)
    r = run_bass_kernel_spmd(nc, [arrays], core_ids=[0])
    return r.results[0]["out"].reshape(BATCHES, SEQ, V)
```
